# Optimizing a Trainium2 kernel written in Bass

```python
import numpy as np
import jax
import jax.numpy as jnp

def _softmax(x, axis=-1):
    return jax.nn.softmax(x, axis=axis)

def _gelu(x):
    return jax.nn.gelu(x, approximate=True)

def _silu(x):
    return jax.nn.silu(x)

def _sigmoid(x):
    return jax.nn.sigmoid(x)

def _layernorm(x, axis=-1, eps=1e-05):
    m = jnp.mean(x, axis=axis, keepdims=True)
    v = jnp.var(x, axis=axis, keepdims=True)
    return (x - m) / jnp.sqrt(v + eps)

def _scatter_add(tgt, idx, src, axis=0):
    return tgt.at[idx].add(src)

def _segment_sum(src, seg, n):
    return jax.ops.segment_sum(src, seg, n)
kernel_name = 'mk_lm_tower_d2_tok_ids256_r4_19b4e0'

def setup_inputs(seed: int=0):
    np.random.seed(seed)
    _w = jnp.asarray

    def _rec_inputs():
        import jax
        import jax.numpy as jnp
        _rk = jax.random.key(seed)
        x = jax.random.randint(jax.random.fold_in(_rk, 1), (16, 128), 0, 75, jnp.int32)
        mask_BS_i0_1 = jnp.where(jnp.ones((16, 128), dtype=bool), 0, 1).astype(jnp.int32)
        itok_BS_0_299 = jax.random.randint(jax.random.fold_in(_rk, 22), (16, 128), 0, 75, jnp.int32)
        return (x, mask_BS_i0_1, itok_BS_0_299)
    x, mask_BS_i0_1, itok_BS_0_299 = _rec_inputs()

    def _L0_tok_setup():
        import jax, jax.numpy as jnp
        import numpy as np
        NUM_SKILLS = 75
        EMB_SIZE = 64
        CURVE_DIM = 64
        B, S = (128, 200)

        def _running_counts(q, r):
            b, s = q.shape
            rows = jnp.arange(b)
            valid = (q >= 0) & (q < NUM_SKILLS)
            idx = jnp.clip(q, 0, NUM_SKILLS - 1)

            def step(carry, xs):
                att, cor = carry
                it, rt, vt = xs
                att = att.at[rows, it].add(vt.astype(jnp.int32))
                cor = cor.at[rows, it].add((rt * vt).astype(jnp.int32))
                return ((att, cor), (att[rows, it], cor[rows, it]))
            init = (jnp.zeros((b, NUM_SKILLS), jnp.int32), jnp.zeros((b, NUM_SKILLS), jnp.int32))
            xs = (idx.T, r.T, valid.T)
            _, (a_t, c_t) = jax.lax.scan(step, init, xs)
            return (a_t.T.astype(jnp.float32), c_t.T.astype(jnp.float32), valid)
        key = jax.random.key(seed)
        ks = jax.random.split(key, 11)
        d3 = CURVE_DIM // 3
        dm = d3 + CURVE_DIM % 3
        return {'q': jax.random.randint(ks[0], (B, S), 0, NUM_SKILLS, dtype=jnp.int32), 'r': jax.random.randint(ks[1], (B, S), 0, 2, dtype=jnp.int32), 'qry': jax.random.randint(ks[2], (B, S), 0, NUM_SKILLS, dtype=jnp.int32), 'skill_w': jax.random.normal(ks[3], (d3,), jnp.float32), 'skill_b': jax.random.normal(ks[4], (d3,), jnp.float32), 'att_w': jax.random.normal(ks[5], (d3,), jnp.float32), 'att_b': jax.random.normal(ks[6], (d3,), jnp.float32), 'mast_w': jax.random.normal(ks[7], (dm,), jnp.float32), 'mast_b': jax.random.normal(ks[8], (dm,), jnp.float32), 'proj_w': jax.random.normal(ks[9], (EMB_SIZE, CURVE_DIM), jnp.float32) * 0.05, 'proj_b': jax.random.normal(ks[10], (EMB_SIZE,), jnp.float32)}
    _L0_tok_all = _L0_tok_setup()
    _L0_tok_in = {k: v for k, v in _L0_tok_all.items() if k in ('skill_w', 'skill_b', 'att_w', 'att_b', 'mast_w', 'mast_b', 'proj_w', 'proj_b')}
    del _L0_tok_all

    def _L0_attn_setup():
        import jax, jax.numpy as jnp
        import numpy as np
        import math
        EMBED_DIMS = 64
        NUM_LANDMARKS = 40
        B, N = (2, 2048)
        key = jax.random.key(seed)
        ks = jax.random.split(key, 9)
        C = EMBED_DIMS
        w = lambda k: jax.random.normal(k, (C, C), dtype=jnp.float32) * 0.02
        b = lambda k: jax.random.normal(k, (C,), dtype=jnp.float32) * 0.02
        return {'query': jax.random.normal(ks[0], (B, N, C), dtype=jnp.float32), 'Wq': w(ks[1]), 'bq': b(ks[2]), 'Wk': w(ks[3]), 'bk': b(ks[4]), 'Wv': w(ks[5]), 'bv': b(ks[6]), 'Wo': w(ks[7]), 'bo': b(ks[8])}
    _L0_attn_all = _L0_attn_setup()
    _L0_attn_in = {k: v for k, v in _L0_attn_all.items() if k in ('Wq', 'bq', 'Wk', 'bk', 'Wv', 'bv', 'Wo', 'bo')}
    del _L0_attn_all

    def _L0_ffn_setup():
        import jax, jax.numpy as jnp
        import numpy as np
        B, T, C = (64, 96, 64)
        NH, NKV = (4, 2)
        HD = C // NH
        NREP = NH // NKV
        NE, TOPK = (8, 2)
        HID = int(8 / 3 * C)
        EPS_RMS = 1e-06

        def _rope_tables(t_len):
            inv_freq = 1.0 / 10000.0 ** (np.arange(0, HD, 2, dtype=np.float32) / HD)
            t = np.arange(t_len, dtype=np.float32)
            freqs = np.outer(t, inv_freq)
            emb = np.concatenate([freqs, freqs], axis=-1)
            return (jnp.asarray(np.cos(emb)), jnp.asarray(np.sin(emb)))

        def _rotate_half(x):
            h = x.shape[-1] // 2
            return jnp.concatenate([-x[..., h:], x[..., :h]], axis=-1)

        def _rmsnorm(v, w):
            return v * jax.lax.rsqrt(jnp.mean(v * v, axis=-1, keepdims=True) + EPS_RMS) * w
        key = jax.random.key(seed)
        ks = jax.random.split(key, 10)
        s = lambda k, shape: jax.random.normal(k, shape, jnp.float32) * 0.02
        return {'x': jax.random.normal(ks[0], (B, T, C), jnp.float32), 'ln1_w': jnp.ones((C,), jnp.float32), 'ln2_w': jnp.ones((C,), jnp.float32), 'wq': s(ks[1], (NH * HD, C)), 'wk': s(ks[2], (NKV * HD, C)), 'wv': s(ks[3], (NKV * HD, C)), 'wo': s(ks[4], (C, C)), 'router_w': s(ks[5], (NE, C)), 'w1': s(ks[6], (NE, HID, C)), 'w2': s(ks[7], (NE, C, HID)), 'w3': s(ks[8], (NE, HID, C))}
    _L0_ffn_all = _L0_ffn_setup()
    _L0_ffn_in = {k: v for k, v in _L0_ffn_all.items() if k in ('ln1_w', 'ln2_w', 'wq', 'wk', 'wv', 'wo', 'router_w', 'w1', 'w2', 'w3')}
    del _L0_ffn_all

    def _L1_attn_setup():
        import jax, jax.numpy as jnp
        import numpy as np
        key = jax.random.key(seed)
        k1, k2, k3 = jax.random.split(key, 3)
        d = 64
        x = jax.random.normal(k1, (8, 512, d), dtype=jnp.float32)
        Wq = jax.random.normal(k2, (d, d), dtype=jnp.float32) * d ** (-0.5)
        Wk = jax.random.normal(k3, (d, d), dtype=jnp.float32) * d ** (-0.5)
        return {'x': x, 'Wq': Wq, 'Wk': Wk}
    _L1_attn_all = _L1_attn_setup()
    _L1_attn_in = {k: v for k, v in _L1_attn_all.items() if k in ('Wq', 'Wk')}
    del _L1_attn_all

    def _L1_ffn_setup():
        import jax, jax.numpy as jnp
        import numpy as np
        E, D, H, TOP_K = (6, 64, 64, 2)
        ROUTER_H = D // 2
        key = jax.random.key(seed)
        ks = jax.random.split(key, 12)
        s = 1.0 / np.sqrt(D)
        sh = 1.0 / np.sqrt(H)
        sr = 1.0 / np.sqrt(ROUTER_H)
        return {'features': jax.random.normal(ks[0], (8, 1024, D), dtype=jnp.float32), 'router_w1': jax.random.uniform(ks[1], (D, ROUTER_H), jnp.float32, -s, s), 'router_b1': jnp.zeros((ROUTER_H,), jnp.float32), 'router_w2': jax.random.uniform(ks[2], (ROUTER_H, E), jnp.float32, -sr, sr), 'router_b2': jnp.zeros((E,), jnp.float32), 'expert_w1': jax.random.uniform(ks[3], (E, D, H), jnp.float32, -s, s), 'expert_b1': jnp.zeros((E, H), jnp.float32), 'expert_w2': jax.random.uniform(ks[4], (E, H, H), jnp.float32, -sh, sh), 'expert_b2': jnp.zeros((E, H), jnp.float32), 'expert_w3': jax.random.uniform(ks[5], (E, H, D), jnp.float32, -sh, sh), 'expert_b3': jnp.zeros((E, D), jnp.float32)}
    _L1_ffn_all = _L1_ffn_setup()
    _L1_ffn_in = {k: v for k, v in _L1_ffn_all.items() if k in ('router_w1', 'router_b1', 'router_w2', 'router_b2', 'expert_w1', 'expert_b1', 'expert_w2', 'expert_b2', 'expert_w3', 'expert_b3')}
    del _L1_ffn_all
    return {'x': x, 'mask_BS_i0_1': mask_BS_i0_1, 'itok_BS_0_299': itok_BS_0_299, 'L0_tok_skill_w': _L0_tok_in['skill_w'], 'L0_tok_skill_b': _L0_tok_in['skill_b'], 'L0_tok_att_w': _L0_tok_in['att_w'], 'L0_tok_att_b': _L0_tok_in['att_b'], 'L0_tok_mast_w': _L0_tok_in['mast_w'], 'L0_tok_mast_b': _L0_tok_in['mast_b'], 'L0_tok_proj_w': _L0_tok_in['proj_w'], 'L0_tok_proj_b': _L0_tok_in['proj_b'], 'L0_attn_Wq': _L0_attn_in['Wq'], 'L0_attn_bq': _L0_attn_in['bq'], 'L0_attn_Wk': _L0_attn_in['Wk'], 'L0_attn_bk': _L0_attn_in['bk'], 'L0_attn_Wv': _L0_attn_in['Wv'], 'L0_attn_bv': _L0_attn_in['bv'], 'L0_attn_Wo': _L0_attn_in['Wo'], 'L0_attn_bo': _L0_attn_in['bo'], 'L0_ffn_ln1_w': _L0_ffn_in['ln1_w'], 'L0_ffn_ln2_w': _L0_ffn_in['ln2_w'], 'L0_ffn_wq': _L0_ffn_in['wq'], 'L0_ffn_wk': _L0_ffn_in['wk'], 'L0_ffn_wv': _L0_ffn_in['wv'], 'L0_ffn_wo': _L0_ffn_in['wo'], 'L0_ffn_router_w': _L0_ffn_in['router_w'], 'L0_ffn_w1': _L0_ffn_in['w1'], 'L0_ffn_w2': _L0_ffn_in['w2'], 'L0_ffn_w3': _L0_ffn_in['w3'], 'L1_attn_Wq': _L1_attn_in['Wq'], 'L1_attn_Wk': _L1_attn_in['Wk'], 'L1_ffn_router_w1': _L1_ffn_in['router_w1'], 'L1_ffn_router_b1': _L1_ffn_in['router_b1'], 'L1_ffn_router_w2': _L1_ffn_in['router_w2'], 'L1_ffn_router_b2': _L1_ffn_in['router_b2'], 'L1_ffn_expert_w1': _L1_ffn_in['expert_w1'], 'L1_ffn_expert_b1': _L1_ffn_in['expert_b1'], 'L1_ffn_expert_w2': _L1_ffn_in['expert_w2'], 'L1_ffn_expert_b2': _L1_ffn_in['expert_b2'], 'L1_ffn_expert_w3': _L1_ffn_in['expert_w3'], 'L1_ffn_expert_b3': _L1_ffn_in['expert_b3']}

def reference(x, mask_BS_i0_1, itok_BS_0_299, L0_tok_skill_w, L0_tok_skill_b, L0_tok_att_w, L0_tok_att_b, L0_tok_mast_w, L0_tok_mast_b, L0_tok_proj_w, L0_tok_proj_b, L0_attn_Wq, L0_attn_bq, L0_attn_Wk, L0_attn_bk, L0_attn_Wv, L0_attn_bv, L0_attn_Wo, L0_attn_bo, L0_ffn_ln1_w, L0_ffn_ln2_w, L0_ffn_wq, L0_ffn_wk, L0_ffn_wv, L0_ffn_wo, L0_ffn_router_w, L0_ffn_w1, L0_ffn_w2, L0_ffn_w3, L1_attn_Wq, L1_attn_Wk, L1_ffn_router_w1, L1_ffn_router_b1, L1_ffn_router_w2, L1_ffn_router_b2, L1_ffn_expert_w1, L1_ffn_expert_b1, L1_ffn_expert_w2, L1_ffn_expert_b2, L1_ffn_expert_w3, L1_ffn_expert_b3):
    import jax
    import jax.numpy as jnp

    def _L0_tok_ref(q, r, qry, skill_w, skill_b, att_w, att_b, mast_w, mast_b, proj_w, proj_b):
        import jax, jax.numpy as jnp
        import numpy as np
        NUM_SKILLS = 75
        EMB_SIZE = 64
        CURVE_DIM = 64
        B, S = (128, 200)

        def _running_counts(q, r):
            b, s = q.shape
            rows = jnp.arange(b)
            valid = (q >= 0) & (q < NUM_SKILLS)
            idx = jnp.clip(q, 0, NUM_SKILLS - 1)

            def step(carry, xs):
                att, cor = carry
                it, rt, vt = xs
                att = att.at[rows, it].add(vt.astype(jnp.int32))
                cor = cor.at[rows, it].add((rt * vt).astype(jnp.int32))
                return ((att, cor), (att[rows, it], cor[rows, it]))
            init = (jnp.zeros((b, NUM_SKILLS), jnp.int32), jnp.zeros((b, NUM_SKILLS), jnp.int32))
            xs = (idx.T, r.T, valid.T)
            _, (a_t, c_t) = jax.lax.scan(step, init, xs)
            return (a_t.T.astype(jnp.float32), c_t.T.astype(jnp.float32), valid)
        attempts, correct, valid = _running_counts(q, r)
        mastery = correct / jnp.maximum(attempts, 1.0)
        skill_f = q.astype(jnp.float32)
        s_enc = skill_f[..., None] * skill_w + skill_b
        n_enc = attempts[..., None] * att_w + att_b
        m_enc = mastery[..., None] * mast_w + mast_b
        tup = jnp.concatenate([s_enc, n_enc, m_enc], axis=-1)
        traj = jnp.einsum('bsc,ec->bse', tup, proj_w) + proj_b
        return jnp.where(valid[..., None], traj, 0.0)

    def _L0_attn_ref(query, Wq, bq, Wk, bk, Wv, bv, Wo, bo):
        import jax, jax.numpy as jnp
        import numpy as np
        import math
        EMBED_DIMS = 64
        NUM_LANDMARKS = 40
        B, N = (2, 2048)
        C = query.shape[-1]
        scaling = math.sqrt(C)
        q = query @ Wq.T + bq
        k = query @ Wk.T + bk
        v = query @ Wv.T + bv
        sim_nm = jnp.einsum('bnc,bmc->bnm', q, k) / scaling
        score_m = sim_nm.sum(axis=1)
        _, top_idx = jax.lax.top_k(score_m, NUM_LANDMARKS)
        selected = jnp.take_along_axis(k, top_idx[:, :, None], axis=1)
        sim_qn = jax.nn.softmax(jnp.einsum('bnc,bkc->bnk', q, selected) / scaling, axis=-1)
        sim_km = jax.nn.softmax(jnp.einsum('bmc,bkc->bmk', k, selected) / scaling, axis=-1)
        sim_qk = jnp.einsum('bnk,bmk->bnm', sim_qn, sim_km)
        out = jnp.einsum('bnm,bmc->bnc', sim_qk, v)
        out = out @ Wo.T + bo
        return query + out

    def _L0_ffn_ref(x, ln1_w, ln2_w, wq, wk, wv, wo, router_w, w1, w2, w3):
        import jax, jax.numpy as jnp
        import numpy as np
        B, T, C = (64, 96, 64)
        NH, NKV = (4, 2)
        HD = C // NH
        NREP = NH // NKV
        NE, TOPK = (8, 2)
        HID = int(8 / 3 * C)
        EPS_RMS = 1e-06

        def _rope_tables(t_len):
            inv_freq = 1.0 / 10000.0 ** (np.arange(0, HD, 2, dtype=np.float32) / HD)
            t = np.arange(t_len, dtype=np.float32)
            freqs = np.outer(t, inv_freq)
            emb = np.concatenate([freqs, freqs], axis=-1)
            return (jnp.asarray(np.cos(emb)), jnp.asarray(np.sin(emb)))

        def _rotate_half(x):
            h = x.shape[-1] // 2
            return jnp.concatenate([-x[..., h:], x[..., :h]], axis=-1)

        def _rmsnorm(v, w):
            return v * jax.lax.rsqrt(jnp.mean(v * v, axis=-1, keepdims=True) + EPS_RMS) * w
        Bx, Tx, Cx = x.shape
        h = _rmsnorm(x, ln1_w)
        q = (h @ wq.T).reshape(Bx, Tx, NH, HD).transpose(0, 2, 1, 3)
        k = (h @ wk.T).reshape(Bx, Tx, NKV, HD).transpose(0, 2, 1, 3)
        v = (h @ wv.T).reshape(Bx, Tx, NKV, HD).transpose(0, 2, 1, 3)
        cos, sin = _rope_tables(Tx)
        cos, sin = (cos[None, None], sin[None, None])
        q = q * cos + _rotate_half(q) * sin
        k = k * cos + _rotate_half(k) * sin
        k = jnp.repeat(k, NREP, axis=1)
        v = jnp.repeat(v, NREP, axis=1)
        scores = jnp.einsum('bhtd,bhsd->bhts', q, k) / jnp.sqrt(jnp.float32(HD))
        causal = jnp.tril(jnp.ones((Tx, Tx), dtype=bool))
        scores = jnp.where(causal[None, None], scores, jnp.float32(-1e+30))
        att = jax.nn.softmax(scores, axis=-1)
        y = jnp.einsum('bhts,bhsd->bhtd', att, v).transpose(0, 2, 1, 3).reshape(Bx, Tx, Cx)
        x = x + y @ wo.T
        flat = _rmsnorm(x, ln2_w).reshape(-1, Cx)
        probs = jax.nn.softmax(flat @ router_w.T, axis=-1)
        tp, ti = jax.lax.top_k(probs, TOPK)
        tp = tp / (jnp.sum(tp, axis=-1, keepdims=True) + 1e-09)
        weights = jnp.sum(tp[..., None] * jax.nn.one_hot(ti, NE, dtype=flat.dtype), axis=1)
        out = jnp.zeros_like(flat)
        for e in range(NE):
            hh = jax.nn.silu(flat @ w1[e].T) * (flat @ w3[e].T)
            out = out + weights[:, e:e + 1] * (hh @ w2[e].T)
        return x + out.reshape(Bx, Tx, Cx)

    def _L1_attn_ref(x, Wq, Wk):
        import jax, jax.numpy as jnp
        import numpy as np
        d = x.shape[-1]
        scale = d ** (-0.5)
        q = jnp.einsum('bnd,ed->bne', x, Wq)
        k = jnp.einsum('bnd,ed->bne', x, Wk)
        sim = jnp.einsum('bid,bjd->bij', q, k) * scale
        attn = jax.nn.softmax(sim, axis=-1)
        out = jnp.einsum('bij,bjd->bid', attn, x)
        return out

    def _L1_ffn_ref(features, router_w1, router_b1, router_w2, router_b2, expert_w1, expert_b1, expert_w2, expert_b2, expert_w3, expert_b3):
        import jax, jax.numpy as jnp
        import numpy as np
        E, D, H, TOP_K = (6, 64, 64, 2)
        ROUTER_H = D // 2
        rh = jax.nn.relu(features @ router_w1 + router_b1)
        expert_logits = jax.nn.softmax(rh @ router_w2 + router_b2, axis=-1)
        top_w, top_i = jax.lax.top_k(expert_logits, TOP_K)
        routing_weights = jax.nn.softmax(top_w, axis=-1)
        h1 = jax.nn.relu(jnp.einsum('bsd,edh->bseh', features, expert_w1) + expert_b1)
        h2 = jax.nn.relu(jnp.einsum('bseh,ehf->bsef', h1, expert_w2) + expert_b2)
        expert_out = jnp.einsum('bsef,efo->bseo', h2, expert_w3) + expert_b3
        sel = jnp.take_along_axis(expert_out, top_i[:, :, :, None], axis=2)
        combined = jnp.sum(sel * routing_weights[..., None], axis=2)
        return combined
    h = _L0_tok_ref(x, mask_BS_i0_1, itok_BS_0_299, L0_tok_skill_w, L0_tok_skill_b, L0_tok_att_w, L0_tok_att_b, L0_tok_mast_w, L0_tok_mast_b, L0_tok_proj_w, L0_tok_proj_b)
    h = h + _L0_attn_ref(_layernorm(h, axis=-1), L0_attn_Wq, L0_attn_bq, L0_attn_Wk, L0_attn_bk, L0_attn_Wv, L0_attn_bv, L0_attn_Wo, L0_attn_bo)
    h = h + _L0_ffn_ref(_layernorm(h, axis=-1), L0_ffn_ln1_w, L0_ffn_ln2_w, L0_ffn_wq, L0_ffn_wk, L0_ffn_wv, L0_ffn_wo, L0_ffn_router_w, L0_ffn_w1, L0_ffn_w2, L0_ffn_w3)
    h = h + _L1_attn_ref(_layernorm(h, axis=-1), L1_attn_Wq, L1_attn_Wk)
    h = h + _L1_ffn_ref(_layernorm(h, axis=-1), L1_ffn_router_w1, L1_ffn_router_b1, L1_ffn_router_w2, L1_ffn_router_b2, L1_ffn_expert_w1, L1_ffn_expert_b1, L1_ffn_expert_w2, L1_ffn_expert_b2, L1_ffn_expert_w3, L1_ffn_expert_b3)
    return h

_drawn_inputs = setup_inputs


def setup_inputs(seed=0):
    import zlib

    import numpy as np

    out = dict(_drawn_inputs(seed))
    spreads = {'L0_ffn_ln1_w': (1.0, 0.6),
     'L0_ffn_ln2_w': (1.0, 0.6),
     'L1_ffn_router_b1': (0.0, 0.8),
     'L1_ffn_router_b2': (0.0, 0.8),
     'L1_ffn_expert_b1': (0.0, 0.8),
     'L1_ffn_expert_b2': (0.0, 0.8),
     'L1_ffn_expert_b3': (0.0, 2.0)}
    factors = {'L0_tok_att_b': 2.983,
     'L0_attn_Wq': 8.0,
     'L0_attn_bq': 8.0,
     'L0_attn_Wk': 8.0,
     'L0_attn_bk': 8.0,
     'L0_attn_Wv': 8.0,
     'L0_attn_bv': 8.0,
     'L0_attn_Wo': 8.0,
     'L0_attn_bo': 8.0,
     'L0_ffn_wq': 8.0,
     'L0_ffn_wk': 8.0,
     'L0_ffn_wv': 8.0,
     'L0_ffn_wo': 8.0,
     'L0_ffn_router_w': 8.0,
     'L0_ffn_w1': 8.0,
     'L0_ffn_w2': 8.0,
     'L0_ffn_w3': 8.0,
     'L1_attn_Wq': 8.0,
     'L1_attn_Wk': 8.0,
     'L1_ffn_router_w1': 8.0,
     'L1_ffn_router_w2': 8.0,
     'L1_ffn_expert_w1': 8.0,
     'L1_ffn_expert_w2': 8.0,
     'L1_ffn_expert_w3': 8.0}
    for name, (base, spread) in spreads.items():
        noise = np.random.default_rng([zlib.crc32(name.encode()), seed]).standard_normal(out[name].shape)
        drawn = base * np.exp(spread * noise) if base else spread * noise
        out[name] = jnp.asarray(drawn.astype(out[name].dtype))
    for name, factor in factors.items():
        out[name] = (out[name] * factor).astype(out[name].dtype)
    return out
```

```python
from collections import namedtuple
from contextlib import ExitStack

import numpy as np

import concourse.bass as bass
from concourse import mybir
from concourse.alu_op_type import AluOpType as ALU

ACT = mybir.ActivationFunctionType
AX = mybir.AxisListType
F32 = mybir.dt.float32
F32R = mybir.dt.float32r
BF16 = mybir.dt.bfloat16
I32 = mybir.dt.int32

P = 128
NB = 16
C = 64
GT = 4
NG = NB // GT
SKILLS = 75
LAND = 40
FEAT = 5
NH, NKV, HD = 4, 2, 16
NE0, HID = 8, 170
REM = HID - P
NCH = 11
NE1 = 6
EPS_LN, EPS_RMS = 1e-5, 1e-6
NEG = -3.0e38
MASKED = -1.0e30

CHUNKS = [("r", 0), ("f", 0), ("f", 1), ("f", 2), ("r", 1), ("f", 3), ("f", 4), ("f", 5), ("r", 2), ("f", 6), ("f", 7)]
CHUNK_AT = {c: n for n, c in enumerate(CHUNKS)}
PAIR_AFTER = [2, 5, 7, 10]
LAST_PAIR = [n // 2 if kind == "f" else min(3 * n + 2, NE0 - 1) // 2 for kind, n in CHUNKS]
ROUTER_OPS = 20
CONST_TOK, CONST_ALL = 11, 22


def layout_of(widths):
    at, out = 0, {}
    for name, width in widths:
        out[name] = (at, at + width)
        at += width
    return out, at


TOK_PARTS, TOK_W = layout_of([("p1", C), ("auga", P), ("augb", P)])
ATT_PARTS, ATT_W = layout_of([("wqT", C), ("wkT", C), ("wvT", C), ("woT", C), ("bq", 1), ("bk", 1), ("bv", 1),
                              ("l1wq", 2 * C), ("l1wk", C)])
FFN_PARTS, FFN_W = layout_of([("wqkv", 2 * C), ("wo", 2 * C), ("router", NE0), ("ln1", 1), ("ln2", 1),
                              ("cos", HD), ("sin", HD)])
MIX_PARTS, MIX_W = layout_of([("rw1", 32), ("ew1", NE1 * C), ("ew2", NE1 * C), ("ew3", NE1 * C), ("eb1", 3), ("eb2", 3),
                              ("rb1", 1), ("rw2", NE1)])


def bank_plan(order):
    uses = [("mct", 0, 1), ("qkv5", 1, 1), ("cnt", 3, 1), ("small", 2, 1),
            ("ut0", 4, 1), ("hc0", 5, 1), ("hc1", 6, 1), ("gT", 7, 1), ("gsum", 0, 1), ("z", 1, 1), ("scT", 2, 1),
            ("posT", 3, 1), ("landq", 4, 1)]
    uses += [(("logit", k), [0, 5, 6, 7][k], 1) for k in range(4)]
    uses += [("gb", 1, 1), (("eqT", 0), 2, 1), (("eqT", 1), 3, 1), ("a", 4, 1), ("ut1", 0, 1), (("h1", 0), 5, 1),
             (("h1", 1), 6, 1), ("l1a", 7, 1)]
    for step, g in order:
        if step == "F0":
            uses += [(("xt", g), 0, 1), (("qkv", g), 1, 2)]
        elif step == "F1":
            uses += [(("qT", g), 2, 1), (("kT", g), 3, 1)]
        elif step == "F2":
            for i in range(GT + 2):
                if i < GT:
                    uses.append((("s", g, i), 4 + i % 2, 1))
                if 1 <= i <= GT:
                    uses.append((("pT", g, i - 1), 6, 1))
                if i == 2:
                    uses.append((("y", g), 7, 1))
        elif step == "F3":
            uses += [(("yT", g), 0, 1), (("proj", g), 1, 1)]
        elif step == "F4":
            uses += [(("xt2", g), 0, 1), (("route", g), 1, 1)]
        elif step == "M0":
            for t in range(NG * NCH + 1):
                if t < NG * NCH:
                    uses += [(("u1", t), 2 * (t % 2), 1), (("u3", t), 2 * (t % 2) + 1, 0)]
                if t and (t - 1) % NCH in PAIR_AFTER:
                    j = PAIR_AFTER.index((t - 1) % NCH)
                    uses.append((("pair", (t - 1) // NCH, j), 4 + j % 2, 1))
        elif step == "A1":
            uses += [(("x3T", g), 6, 1), (("u", g), 7, 1), (("sim", g), 5, 1)]
        elif step == "A2":
            uses += [(("p1T", g), 6, 1), (("o1", g), 7, 1)]
        elif step == "M1":
            uses += [(("xt3", g), 0, 1), (("rh", g), 1, 1), (("route1", g), 1, 1)]
        elif step == "M2":
            for c in range(3):
                uses += [(("h1c", g, c), 2, 1)] if c == 0 else []
                uses += [(("h1c", g, c + 1), 2, 1)] if c < 2 else []
                uses += [(("h2c", g, c), 3, 1), (("oc", g, c), (4, 1)[c % 2], 1)]
    bank, full, free, done = {}, {}, {}, {}
    written, read = [0] * 8, [0] * 8
    for key, b, readers in uses:
        assert key not in bank, key
        bank[key] = b
        free[key] = read[b]
        written[b] += 0 if key[0] == "y" else 1
        read[b] += readers
        full[key], done[key] = written[b], read[b]
    return bank, full, free, done


def steps_of(order, *names):
    return [g for step, g in order if step in names]


ORDER = [("F0", 0), ("F1", 0), ("F0", 1), ("F1", 1), ("F2", 0), ("F3", 0), ("F0", 2), ("F1", 2), ("F4", 0), ("F2", 1),
         ("F3", 1), ("F0", 3), ("F1", 3), ("F4", 1), ("F2", 2), ("F3", 2), ("F4", 2), ("F2", 3), ("F3", 3), ("F4", 3),
         ("M0", 0),
         ("A1", 0), ("A2", 0), ("A1", 1), ("M1", 0), ("A2", 1), ("A1", 2), ("M2", 0), ("M1", 1), ("A2", 2), ("A1", 3),
         ("M2", 1), ("M1", 2), ("A2", 3), ("M2", 2), ("M1", 3), ("M2", 3)]


def tower_program(nc, x_row, x_col, mask_col, tokw, attw, ffnw, w13, w2, mixw, eb3, out):
    bank, full, free, done = bank_plan(ORDER)
    ctx = ExitStack()
    with ctx:
        def sb(name, shape, dt=F32):
            return ctx.enter_context(nc.sbuf_tensor(name, shape, dt))

        xcol_i = sb("xcol_i", [P, NB], I32)
        mcol_i = sb("mcol_i", [P, NB], I32)
        tok_w = sb("tok_w", [C + 2, TOK_W])
        att_w = sb("att_w", [C, ATT_W])
        ffn_w = sb("ffn_w", [P, FFN_W])
        mix_w = sb("mix_w", [P, MIX_W])
        later = sb("later", [P, 7 * 512])
        w13_raw = later[:, 0:2 * NCH * P]
        w2_sb = sb("w2_sb", [P, 2 * 512])
        b3_raw = sb("b3_raw", [33, NE1 * C])

        arena = sb("arena", [P, 12 * 512])
        work = [arena[:, 512 * i:512 * i + 512] for i in range(12)]

        def early(lo, *shape):
            flat = arena[:, lo:lo + int(np.prod(shape))]
            if len(shape) == 2:
                return flat.rearrange("p (a b) -> p a b", a=shape[0])
            return flat

        ident = sb("ident", [P, P])
        ident_b = sb("ident_b", [P, P], BF16)
        ones = sb("ones", [P, P])
        causal_T = sb("causal_T", [P, P])
        neg_mask = sb("neg_mask", [P, GT, P], BF16)
        own_block = sb("own_block", [P, 8])
        own_quarter = sb("own_quarter", [P, GT])
        rank_iota = sb("rank_iota", [P, LAND])
        rev_iota = sb("rev_iota", [P, 8])
        half_neg = sb("half_neg", [P, NB])
        ones33 = sb("ones33", [33, P], F32R)

        p1c = sb("p1c", [C + 1, C])
        rowsum = sb("rowsum", [C + 1, 2])
        mct = sb("mct", [C, 4])
        qk5 = sb("qk5", [C, 2 * FEAT])
        k5_pad = sb("k5_pad", [C, GT, 32])
        v5_pad = sb("v5_pad", [C, 8, 16])
        k10 = sb("k10", [P, GT, 2 * FEAT])
        wc_blk = sb("wc_blk", [P, 8, C])
        w16_blk = sb("w16_blk", [P, 8, C])
        l1a = sb("l1a", [P, C])
        qkv_s = sb("qkv_s", [P, 2 * C])
        qkv_h = sb("qkv_h", [P, 2 * C], F32R)
        qkv_l = sb("qkv_l", [P, 2 * C], F32R)
        rt_s = sb("rt_s", [P, NE0])
        rt_h = sb("rt_h", [P, NE0], F32R)
        rt_l = sb("rt_l", [P, NE0], F32R)
        w13_h = sb("w13_h", [P, 2 * NCH * P], F32R)
        w13_l = sb("w13_l", [P, 2 * NCH * P], F32R)
        ew_h = sb("ew_h", [P, 32 + NE1 * C], F32R)
        ew_l = sb("ew_l", [P, 32 + NE1 * C], F32R)
        b3_hl = sb("b3_hl", [33, NE1 * C], F32R)
        b3_h = sb("b3_h", [33, NE1 * C], F32R)

        h1 = sb("h1", [P, NB, C])
        h2 = sb("h2", [P, NB, C])
        h3 = sb("h3", [P, NB, C])
        xcol = sb("xcol", [P, NB])
        valid = sb("valid", [P, NB, 2])
        xrow_i = early(0, NB * P).bitcast(I32)
        same = early(2048, NB, P)
        one_r = sb("one_r", [P, NB, 2])
        cnt = sb("cnt", [P, NB, 2])
        mast = sb("mast", [P, NB, 2])
        feats = sb("feats", [P, NB, 16])
        feats_T = sb("feats_T", [P, 2, P])
        feats_T1 = sb("feats_T1", [P, 2, P])
        hsq = early(4096, NB, C)
        var0 = sb("var0", [P, NB])
        var0e = sb("var0e", [P, NB])
        inv0 = sb("inv0", [P, NB])
        g5 = h2[:, 0:8].rearrange("p a b -> p (a b)").rearrange("p (a b) -> p a b", b=32)
        g5_T = h2[:, 8:16].rearrange("p a b -> p (a b)").rearrange("p (a b) -> p a b", b=P)
        z = h3[:].rearrange("p a b -> p (a b)").rearrange("p (k a b) -> p k a b", k=2, b=32)
        zg = sb("zg", [P, NB, FEAT])
        score = sb("score", [P, NB])
        score_T = early(3584, 6, P)[0:NB]
        top8 = sb("top8", [NB, 5, 8])
        chosen = sb("chosen", [NB, P])
        ones16 = sb("ones16", [NB, P])
        count_T = sb("count_T", [NB, P])
        place_T = sb("place_T", [NB, P])
        pick = early(0, NB, LAND)
        y10 = early(4352, GT, 2 * LAND)
        lmax = sb("lmax", [P, GT, 8])
        lsub = early(2304, 32, LAND).rearrange("p (i r) l -> p i r l", i=GT)
        eq = early(5120, NB, 64)
        ek = early(640, NB, LAND)
        lsum = sb("lsum", [P, 2, NB])
        linv = sb("linv", [P, 2, NB])
        g5k = sb("g5k", [P, NB, FEAT])
        eq_T = early(1280, 8, P)
        gsum_l = sb("gsum_l", [P, 8, 2, FEAT])

        h12 = sb("h12", [P, NB, C])
        h4 = h12

        def per_group(name, shape, dt=F32):
            t = sb(name, [shape[0], NG] + shape[1:], dt)
            return [t[:, g] for g in range(NG)]

        nsum = [per_group(f"nsum{n}", [P, GT]) for n in range(4)]
        ncen = [per_group("ncen", [P, GT, C])] * 4
        nss = [per_group(f"nss{n}", [P, GT]) for n in range(4)]
        nve = [per_group(f"nve{n}", [P, 2, GT]) for n in range(4)]
        ninv = [per_group(f"ninv{n}", [P, 2, GT]) for n in range(4)]
        xhl = [per_group("xhl", [P, GT, 2, C], F32R)] * 3
        xT = [per_group(f"xT{n}", [P, GT, P], F32R) for n in range(2)]
        xT.append(xT[0])
        x2 = per_group("x2", [P, GT, C])
        shared = sb("shared", [P, 6 * 512])
        half = GT * 6 * HD
        rope1, rope2 = ([shared[:, half * (2 * g + k):half * (2 * g + k + 1)].rearrange("p (t h d) -> p t h d", t=GT, h=6)
                         for g in range(NG)] for k in range(2))
        q_pad = [sb(f"q_pad{i}", [P, GT, NH, 32]) for i in range(2)]
        k_pad = [sb(f"k_pad{i}", [P, GT, NKV, 2, 32]) for i in range(2)]
        v1 = per_group("v1", [P, GT, NKV, HD + 1])
        qT = [sb(f"qT{i}", [P, GT, P]) for i in range(2)]
        kT = [sb(f"kT{i}", [P, GT, P]) for i in range(2)]
        smax = per_group("smax", [P, NH, GT])
        probs = [work[i].rearrange("p (t s) -> p t s", t=GT) for i in range(4)]
        expd = [work[4 + i].rearrange("p (t s) -> p t s", t=GT) for i in range(4)]
        probs_T = [work[8 + i].rearrange("p (t s) -> p t s", t=GT) for i in range(4)]
        yinv = per_group("yinv", [P, GT * NH])
        ynorm = per_group("ynorm", [P, GT, C])
        yT = per_group("yT", [P, 2, P])
        nsq = [[v.rearrange("p a b -> p (a b)").rearrange("p (t c) -> p t c", t=GT) for v in yT]] * 4
        xs = [ynorm] * 3
        xres = ncen[0]

        route_cols = {n: per_group(f"route_{n}", [P, GT]) for n in "lmax s inv best1 max2 best2 sum2 den deni".split()}
        route_rows = {n: per_group(f"route_{n}", [P, GT, NE0])
                      for n in "lsub ex p eq1 key1 one1 rest eq2 key2 one2 both pw sub2 ex2 w".split()}

        RouterArrays = namedtuple("RouterArrays", [*route_cols, *route_rows])

        def router_set(e):
            return RouterArrays(*route_cols.values(), *([v[:, :, 0:e] for v in t] for t in route_rows.values()))

        rs = [router_set(NE0), router_set(NE1)]

        gate = [later[:, 2048 + 512 * i:2560 + 512 * i] for i in range(3)]
        hid = work[0:NCH]
        weighted = [later[:, 512 * i:512 * i + 512].rearrange("p (t e c) -> p t e c", t=GT, e=2) for i in range(4)]
        acc = [shared[:, 512 * g:512 * g + 512].rearrange("p (t e c) -> p t e c", t=GT, e=2) for g in range(NG)]
        folded = [shared[:, 2048 + 256 * g:2304 + 256 * g].rearrange("p (t c) -> p t c", t=GT) for g in range(NG)]

        x3 = per_group("x3", [P, GT, C])
        x3T = [x2[g].rearrange("p t c -> p (t c)").rearrange("p (a b) -> p a b", a=2) for g in range(NG)]
        uT = yT
        m1 = per_group("m1", [P, GT])
        p1 = [work[i].rearrange("p (t s) -> p t s", t=GT) for i in range(2)]
        e1 = [work[2 + i].rearrange("p (t s) -> p t s", t=GT) for i in range(2)]
        p1T = [work[4 + i].rearrange("p (t s) -> p t s", t=GT) for i in range(2)]
        o1inv = per_group("o1inv", [P, GT])
        o1 = ynorm
        rh = [sb(f"rh{i}", [33, 512])[:] for i in range(2)] * 2
        hid1 = work[6:8]
        hid2 = work[8:10]
        weighted1 = weighted
        acc1 = acc

        ps = [ctx.enter_context(nc.psum_tensor(f"bank{b}", [P, 512], F32)) for b in range(8)]

        def at(key):
            return ps[bank[key]]

        def sems(names):
            return namedtuple("Semaphores", names)(*(ctx.enter_context(nc.semaphore(n)) for n in names.split()))

        bank_full = [ctx.enter_context(nc.semaphore(f"bank_full{b}")) for b in range(8)]
        bank_free = [ctx.enter_context(nc.semaphore(f"bank_free{b}")) for b in range(8)]
        s = sems("tok_in tokw_in attw_in ffnw_in mixw_in w13_in w2_in b3_in stored "
                 "zeros shapes const p1c_ok mct_ok five_ok k10_ok wcblk_ok "
                 "folded_ok proj_hi proj_lo w13_scaled w13_hi w13_lo ew_hi ew_lo b3_hi "
                 "xc vld same_ok one_r_ok mst feats_ok var0_ok inv0_ok g5_ok "
                 "score_ok topk chosen_ok count_ok place_ok lmax_ok eexp lsum_ok linv_ok g5k_ok attended "
                 "nsum_ok ncen_ok nsq_ok nss_ok nve_ok ninv_ok xs_ok xhi_ok xlo_ok x2_ok "
                 "qkpad_ok smax_ok sexp_ok yinv_ok pv_done "
                 "router0 router1 route_exp0 route_exp1 hid_ok acc0_ok acc1_ok h12_ok fold0_ok fold1_ok h2_ok "
                 "sim_half x3_ok m1_ok e1_ok o1inv_ok h3_ok h4_ok")

        def wait_full(eng, key):
            eng.wait_ge(bank_full[bank[key]], full[key])

        def wait_free(eng, key):
            if free[key]:
                eng.wait_ge(bank_free[bank[key]], free[key])

        def wait_read(eng, key):
            eng.wait_ge(bank_free[bank[key]], done[key])

        def written(ins, key):
            ins.then_inc(bank_full[bank[key]], 1)

        def read(ins, key):
            ins.then_inc(bank_free[bank[key]], 1)

        def grp(t, g):
            return t[:, GT * g:GT * g + GT]

        def bc(ap, n):
            k = len(ap.shape)
            return ap.unsqueeze(k).to_broadcast(list(ap.shape) + [n])

        def bc_mid(ap, n):
            return ap.unsqueeze(1).to_broadcast([ap.shape[0], n] + list(ap.shape[1:]))

        def tokp(name, rows=C + 2):
            a, b = TOK_PARTS[name]
            return tok_w[0:rows, a:b]

        def attp(name):
            a, b = ATT_PARTS[name]
            return att_w[:, a:b]

        def ffnp(name):
            a, b = FFN_PARTS[name]
            return ffn_w[:, a:b]

        def mixp(name, rows=P):
            a, b = MIX_PARTS[name]
            return mix_w[0:rows, a:b]

        norm_of = {"F0": 0, "F4": 1, "A1": 2, "M1": 3}
        norms = [(norm_of[step], g) for step, g in ORDER if step in norm_of]
        squared = [({"F3": 1} | norm_of)[step] * NG + g for step, g in ORDER if step in ("F0", "F3", "A1", "M1")]
        norm_turn = {divmod(k, NG): n + 1 for n, k in enumerate(squared)}
        inv_turn = {k: n + 1 for n, k in enumerate(norms)}
        centre_turn = {k: n + 1 for n, k in enumerate(k for k in norms if k[0] != 1)}
        split_turn = {k: n + 1 for n, k in enumerate(k for k in norms if k[0] != 2)}
        split_of = {0: 0, 1: 1, 3: 2}

        block = ctx.enter_context(nc.Block())

        @block.sync
        def _(sp):
            sp.dma_start(xcol_i[:], x_col).then_inc(s.tok_in, 16)
            sp.dma_start(xrow_i, x_row.partition_broadcast(P)).then_inc(s.tok_in, 16)
            sp.dma_start(mcol_i[:], mask_col).then_inc(s.tok_in, 16)
            sp.dma_start(ffn_w[:], ffnw).then_inc(s.ffnw_in, 16)
            sp.dma_start(w13_raw, w13).then_inc(s.w13_in, 16)
            sp.dma_start(w2_sb[:], w2).then_inc(s.w2_in, 16)
            for step, g in ORDER:
                if step == "M2":
                    sp.wait_ge(s.h4_ok, g + 1)
                    sp.dma_start(out[GT * g:GT * g + GT].rearrange("b t c -> t b c"), grp(h4, g)).then_inc(s.stored, 16)
            sp.wait_ge(s.stored, 16 * NG)

        @block.gpsimd
        def _(pool):
            pool.memset(ident[:], 0.0).then_inc(s.zeros, 1)
            pool.memset(ones[:], 1.0).then_inc(s.zeros, 1)
            pool.memset(neg_mask[:], 0.0).then_inc(s.zeros, 1)
            pool.memset(half_neg[:], -0.5).then_inc(s.zeros, 1)
            pool.wait_ge(s.zeros, 2)
            pool.affine_select(out=causal_T[:], in_=ones[:], compare_op=ALU.is_ge, fill=0.0, base=0,
                               pattern=[[1, P]], channel_multiplier=-1).then_inc(s.shapes, 1)
            pool.affine_select(out=ident[:], in_=ident[:], compare_op=ALU.not_equal, fill=1.0, base=0,
                               pattern=[[-1, P]], channel_multiplier=1).then_inc(s.shapes, 1)
            pool.affine_select(out=own_block[:], in_=ones[:, 0:8], compare_op=ALU.is_ge, fill=0.0, base=0,
                               pattern=[[-16, 8]], channel_multiplier=1).then_inc(s.shapes, 1)
            pool.affine_select(out=own_quarter[:], in_=ones[:, 0:GT], compare_op=ALU.is_ge, fill=0.0, base=0,
                               pattern=[[-32, GT]], channel_multiplier=1).then_inc(s.shapes, 1)
            pool.wait_ge(s.shapes, 4)
            pool.affine_select(out=own_block[:], in_=own_block[:], compare_op=ALU.is_ge, fill=0.0, base=15,
                               pattern=[[16, 8]], channel_multiplier=-1).then_inc(s.shapes, 1)
            pool.affine_select(out=own_quarter[:], in_=own_quarter[:], compare_op=ALU.is_ge, fill=0.0, base=31,
                               pattern=[[32, GT]], channel_multiplier=-1).then_inc(s.shapes, 1)
            pool.tensor_copy(ident_b[:], ident[:]).then_inc(s.const, 1)
            pool.wait_ge(s.zeros, 4)
            pool.affine_select(out=neg_mask[:], in_=neg_mask[:], compare_op=ALU.is_ge, fill=MASKED, base=0,
                               pattern=[[0, GT], [-1, P]], channel_multiplier=1).then_inc(s.const, 1)
            pool.iota(rank_iota[:], pattern=[[1, LAND]], base=1, channel_multiplier=0,
                      allow_small_or_imprecise_dtypes=True).then_inc(s.const, 1)
            pool.iota(rev_iota[:], pattern=[[-1, 8]], base=8, channel_multiplier=0,
                      allow_small_or_imprecise_dtypes=True).then_inc(s.const, 1)
            pool.tensor_copy(ones33[:], ones[0:33, :]).then_inc(s.const, 1)
            for t in (k5_pad[:], v5_pad[:], feats[:], g5, z, eq, gsum_l[:], q_pad[0][:], q_pad[1][:], k_pad[0][:], k_pad[1][:],
                      b3_raw[:], b3_hl[:].bitcast(F32)):
                pool.memset(t, 0.0).then_inc(s.const, 1)
            for g in range(NG):
                pool.memset(v1[g][:, :, :, HD:HD + 1], 1.0).then_inc(s.const, 1)
            pool.wait_ge(s.const, CONST_ALL)
            for row in (0, 32):
                pool.dma_start(b3_raw[row:row + 1, :], eb3).then_inc(s.b3_in, 16)
            pool.wait_ge(s.var0_ok, 1)
            pool.tensor_scalar(var0e[:], var0[:], 1.0 / C, EPS_LN, ALU.mult, ALU.add).then_inc(s.inv0_ok, 1)
            pool.wait_ge(s.inv0_ok, 1)
            pool.tensor_tensor(inv0[:], var0e[:], half_neg[:], ALU.pow).then_inc(s.inv0_ok, 1)

            def inverse_root(n, g):
                t = inv_turn[n, g]
                pool.wait_ge(s.nss_ok, norm_turn[n, g])
                eps = EPS_RMS if n == 1 else EPS_LN
                ins = pool.tensor_scalar(nve[n][g][:, 0], nss[n][g], 1.0 / C, eps, ALU.mult, ALU.add)
                if n == 0:
                    ins = pool.tensor_scalar(nve[n][g][:, 1], nss[n][g], (1.0 + EPS_RMS) / C, EPS_LN * EPS_RMS, ALU.mult,
                                             ALU.add)
                ins.then_inc(s.nve_ok, 1)
                pool.wait_ge(s.nve_ok, t)
                k = 2 if n == 0 else 1
                pool.tensor_tensor(ninv[n][g][:, 0:k].rearrange("p a b -> p (a b)"),
                                   nve[n][g][:, 0:k].rearrange("p a b -> p (a b)"),
                                   half_neg[:, 0:k * GT], ALU.pow).then_inc(s.ninv_ok, 1)

            for step, g in ORDER:
                if step == "F0":
                    inverse_root(0, g)
                elif step == "F1":
                    wait_read(pool, ("qkv", g))
                    if g >= 2:
                        wait_full(pool, ("qT", g - 2))
                        wait_full(pool, ("kT", g - 2))
                    pool.tensor_tensor(q_pad[g % 2][:, :, :, 0:HD], rope1[g][:, :, 0:NH], rope2[g][:, :, 0:NH], ALU.add)
                    for r in range(2):
                        ins = pool.tensor_tensor(k_pad[g % 2][:, :, :, r, 0:HD], rope1[g][:, :, NH:6], rope2[g][:, :, NH:6],
                                                 ALU.add)
                    ins.then_inc(s.qkpad_ok, 1)
                elif step == "F4":
                    inverse_root(1, g)
                    pool.tensor_tensor(grp(h12, g), grp(h1, g), xres[g], ALU.add).then_inc(s.h12_ok, 1)
                elif step == "M0":
                    for q in range(NG):
                        for j in range(1, 4):
                            wait_read(pool, ("pair", q, j))
                            if j > 1:
                                pool.wait_ge(s.acc0_ok, 3 * q + j - 1)
                            pool.tensor_tensor(acc[q], weighted[0] if j == 1 else acc[q], weighted[j],
                                               ALU.add).then_inc(s.acc0_ok, 1)
                elif step == "A1":
                    inverse_root(2, g)
                elif step == "A2":
                    wait_read(pool, ("o1", g))
                    pool.tensor_tensor(grp(h3, g), grp(h2, g), o1[g], ALU.add).then_inc(s.h3_ok, 1)
                elif step == "M1":
                    inverse_root(3, g)
                elif step == "M2":
                    for c in range(1, 3):
                        wait_read(pool, ("oc", g, c))
                        if c > 1:
                            pool.wait_ge(s.acc1_ok, 2 * g + c - 1)
                        pool.tensor_tensor(acc1[g], weighted1[0] if c == 1 else acc1[g], weighted1[c],
                                           ALU.add).then_inc(s.acc1_ok, 1)

        @block.scalar
        def _(act):
            act.dma_start(tok_w[:], tokw).then_inc(s.tokw_in, 16)
            act.dma_start(att_w[:], attw).then_inc(s.attw_in, 16)
            act.dma_start(mix_w[:], mixw).then_inc(s.mixw_in, 16)

            def copy(dst, src):
                return act.activation(dst, src, ACT.Copy)

            wait_full(act, "mct")
            read(copy(mct[:], at("mct")[0:C, 0:4]), "mct")
            act.wait_ge(s.attw_in, 16)
            act.wait_ge(s.const, CONST_TOK)
            wait_full(act, "qkv5")
            q5, k5, v5 = (at("qkv5")[0:C, 8 * n:8 * n + 4] for n in range(3))
            copy(qk5[:, 0:4], q5)
            copy(qk5[:, 4:5], attp("bq"))
            copy(qk5[:, 5:9], k5)
            copy(qk5[:, 9:10], attp("bk"))
            copy(k5_pad[:, :, 0:4], bc_mid(k5, GT))
            copy(k5_pad[:, :, 4:5], bc_mid(attp("bk"), GT))
            copy(v5_pad[:, :, 12:13], bc_mid(attp("bv"), 8))
            read(copy(v5_pad[:, :, 8:12], bc_mid(v5, 8)), "qkv5")
            act.wait_ge(s.ffnw_in, 16)
            act.activation(qkv_s[:], ffnp("wqkv"), ACT.Copy, scale=ffnp("ln1"))
            act.activation(rt_s[:], ffnp("router"), ACT.Copy, scale=ffnp("ln2")).then_inc(s.folded_ok, 1)
            act.wait_ge(s.folded_ok, 1)
            copy(qkv_h[:], qkv_s[:])
            copy(rt_h[:], rt_s[:]).then_inc(s.proj_hi, 1)
            wait_full(act, "ut0")
            copy_t = copy(feats_T[:].rearrange("p a b -> p (a b)"), at("ut0")[:, 0:2 * P])
            read(copy_t, "ut0")
            for k in range(2):
                wait_full(act, f"hc{k}")
                read(act.activation(hsq[:, 8 * k:8 * k + 8].rearrange("p a b -> p (a b)"), at(f"hc{k}")[:], ACT.Square),
                     f"hc{k}")
            wait_full(act, "gT")
            read(copy(g5_T.rearrange("p a b -> p (a b)"), at("gT")[:]), "gT")
            act.wait_ge(s.w13_in, 16)
            for k in range(2):
                part = slice(k * NCH * P, (k + 1) * NCH * P)
                act.activation(w13_raw[:, part], w13_raw[:, part], ACT.Copy, scale=ffnp("ln2")).then_inc(s.w13_scaled, 1)
                act.wait_ge(s.w13_scaled, k + 1)
                copy(w13_h[:, part], w13_raw[:, part]).then_inc(s.w13_hi, 1)
            act.wait_ge(s.mixw_in, 16)
            copy(ew_h[:], mix_w[:, 0:32 + NE1 * C]).then_inc(s.ew_hi, 1)
            act.wait_ge(s.b3_in, 32)
            copy(b3_h[:], b3_raw[:]).then_inc(s.b3_hi, 1)
            wait_full(act, "landq")
            read(copy(y10.rearrange("p a b -> p (a b)"), at("landq")[:, 16:16 + GT * 2 * LAND]), "landq")
            for k in range(4):
                wait_read(act, ("logit", k))
            lv = lsub.rearrange("p i (q two) l -> p q i two l", two=2)
            act.activation(eq[:, :, 0:LAND].rearrange("p (q i) l -> p q i l", i=GT), lv[:, :, :, 0], ACT.Exp, scale=0.125)
            act.activation(ek.rearrange("p (q i) l -> p q i l", i=GT), lv[:, :, :, 1], ACT.Exp, scale=0.125).then_inc(s.eexp, 1)
            for k in range(2):
                wait_full(act, ("eqT", k))
                read(copy(eq_T[:, 4 * k:4 * k + 4].rearrange("p a b -> p (a b)"), at(("eqT", k))[:]), ("eqT", k))
            wait_full(act, "ut1")
            read(copy(feats_T1[:].rearrange("p a b -> p (a b)"), at("ut1")[:, 0:2 * P]), "ut1")
            wait_full(act, ("h1", 1))
            read(copy(h1[:, 8:16].rearrange("p a b -> p (a b)"), at(("h1", 1))[:]), ("h1", 1))
            wait_full(act, "l1a")
            read(copy(l1a[:], at("l1a")[:, 0:C]), "l1a")

            def squares(n, g):
                if n == 1:
                    wait_read(act, ("proj", g))
                else:
                    act.wait_ge(s.ncen_ok, centre_turn[n, g])
                act.activation(nsq[n][g], xres[g] if n == 1 else ncen[n][g], ACT.Square).then_inc(s.nsq_ok, 1)

            def hi_part(n, g):
                k = split_of[n]
                act.wait_ge(s.xs_ok, split_turn[n, g])
                copy(xhl[k][g][:, :, 0], xs[k][g]).then_inc(s.xhi_ok, 1)

            def out_of(dst, key, cols=512):
                wait_full(act, key)
                read(copy(dst.rearrange("p a b -> p (a b)"), at(key)[:, 0:cols]), key)

            for step, g in ORDER:
                if step == "F0":
                    squares(0, g)
                    hi_part(0, g)
                    out_of(xT[0][g], ("xt", g))
                    wait_full(act, ("qkv", g))
                    if g == 0:
                        act.wait_ge(s.const, CONST_ALL)
                    vv = at(("qkv", g))[:].rearrange("p (t c) -> p t c", t=GT)[:, :, 96:128]
                    copy(v1[g][:, :, 0, 0:HD], vv[:, :, 0:HD])
                    read(copy(v1[g][:, :, 1, 0:HD], vv[:, :, HD:2 * HD]), ("qkv", g))
                elif step == "F1":
                    if g >= 2:
                        act.wait_ge(s.pv_done, GT * (g - 1))
                    out_of(qT[g % 2][:], ("qT", g))
                elif step == "F2":
                    for i in range(GT + 1):
                        if i < GT:
                            t = GT * g + i
                            wait_read(act, ("s", g, i))
                            if t >= 4:
                                wait_full(act, ("pT", g - 1, i))
                            act.activation(expd[t % 4], probs[t % 4], ACT.Exp, scale=HD ** -0.5).then_inc(s.sexp_ok, 1)
                        if i >= 1:
                            t = GT * g + i - 1
                            if t >= 4:
                                act.wait_ge(s.pv_done, t - 3)
                            out_of(probs_T[t % 4], ("pT", g, i - 1))
                elif step == "F3":
                    out_of(yT[g], ("yT", g), 2 * P)
                    squares(1, g)
                elif step == "F4":
                    hi_part(1, g)
                    out_of(xT[1][g], ("xt2", g))
                    wait_read(act, ("route", g))
                    act.activation(rs[0].ex[g], rs[0].lsub[g], ACT.Exp).then_inc(s.route_exp0, 1)
                elif step == "M0":
                    for t in range(NG * NCH):
                        wait_full(act, ("u1", t))
                        if t >= 3:
                            act.wait_ge(s.hid_ok, t - 2)
                        read(act.activation(gate[t % 3], at(("u1", t))[:], ACT.Silu), ("u1", t))
                elif step == "A1":
                    squares(2, g)
                    out_of(x3T[g], ("x3T", g), 2 * P)
                    out_of(uT[g], ("u", g), 2 * P)
                elif step == "A2":
                    wait_read(act, ("sim", g))
                    if g >= 2:
                        wait_full(act, ("p1T", g - 2))
                    act.activation(e1[g % 2], p1[g % 2], ACT.Exp, scale=0.125).then_inc(s.e1_ok, 1)
                    if g >= 2:
                        wait_full(act, ("o1", g - 2))
                    out_of(p1T[g % 2], ("p1T", g))
                elif step == "M1":
                    squares(3, g)
                    hi_part(3, g)
                    out_of(xT[2][g], ("xt3", g))
                    wait_full(act, ("rh", g))
                    if g >= 2:
                        wait_full(act, ("route1", g - 2))
                    read(act.activation(rh[g][0:32, :], at(("rh", g))[0:32, :], ACT.Relu, bias=mixp("rb1", 32)), ("rh", g))
                    wait_read(act, ("route1", g))
                    act.activation(rs[1].ex[g], rs[1].lsub[g], ACT.Exp).then_inc(s.route_exp1, 1)
                    act.wait_ge(s.router1, ROUTER_OPS * g + 15)
                    act.activation(rs[1].ex2[g], rs[1].sub2[g], ACT.Exp).then_inc(s.route_exp1, 1)
                elif step == "M2":
                    for c in range(3):
                        wait_full(act, ("h1c", g, c))
                        t = 3 * g + c
                        if t >= 2:
                            wait_full(act, ("h2c",) + divmod(t - 2, 3))
                        read(act.activation(hid1[t % 2], at(("h1c", g, c))[:], ACT.Relu,
                                            bias=mixp("eb1")[:, c:c + 1]), ("h1c", g, c))

        @block.vector
        def _(dve):
            tt = dve.tensor_tensor
            for g in range(2):
                dve.memset(rh[g][32:33, :], 1.0)
            dve.wait_ge(s.tokw_in, 16)
            dve.tensor_reduce(rowsum[:, 0:1], tokp("p1", C + 1), AX.X, ALU.add).then_inc(s.p1c_ok, 1)
            dve.wait_ge(s.p1c_ok, 1)
            dve.tensor_scalar(rowsum[:, 1:2], rowsum[:, 0:1], -1.0 / C, None, ALU.mult).then_inc(s.p1c_ok, 1)
            dve.wait_ge(s.p1c_ok, 2)
            dve.tensor_scalar(p1c[:], tokp("p1", C + 1), rowsum[:, 1:2], None, ALU.add).then_inc(s.p1c_ok, 1)
            dve.wait_ge(s.tok_in, 48)
            dve.tensor_copy(xcol[:], xcol_i[:]).then_inc(s.xc, 1)
            dve.tensor_copy(one_r[:, :, 1], mcol_i[:]).then_inc(s.one_r_ok, 1)
            dve.memset(one_r[:, :, 0], 1.0).then_inc(s.one_r_ok, 1)
            dve.wait_ge(s.xc, 1)
            dve.wait_ge(s.shapes, 6)
            for b in range(NB):
                dve.scalar_tensor_tensor(out=same[:, b], in0=xrow_i[:, P * b:P * b + P], scalar=xcol[:, b:b + 1],
                                         in1=causal_T[:], op0=ALU.is_equal, op1=ALU.mult).then_inc(s.same_ok, 1)
            dve.tensor_scalar(valid[:, :, 0], xcol[:], 0.0, None, ALU.is_ge).then_inc(s.vld, 1)
            dve.wait_ge(s.vld, 1)
            dve.scalar_tensor_tensor(out=valid[:, :, 1], in0=xcol[:], scalar=float(SKILLS), in1=valid[:, :, 0],
                                     op0=ALU.is_lt, op1=ALU.mult).then_inc(s.vld, 1)
            dve.wait_ge(s.vld, 2)
            ok = valid[:, :, 1]
            dve.wait_ge(s.const, CONST_TOK)
            tt(feats[:, :, 0], xcol[:], ok, ALU.mult)
            dve.tensor_copy(feats[:, :, 3], ok)
            wait_full(dve, "cnt")
            read(dve.tensor_copy(cnt[:].rearrange("p a b -> p (a b)"), at("cnt")[:, 0:2 * NB]), "cnt")
            wait_read(dve, "cnt")
            dve.tensor_scalar(mast[:, :, 0], cnt[:, :, 0], 1.0, None, ALU.max).then_inc(s.mst, 1)
            tt(feats[:, :, 1], cnt[:, :, 0], ok, ALU.mult)
            dve.wait_ge(s.mst, 1)
            dve.reciprocal(mast[:, :, 1], mast[:, :, 0]).then_inc(s.mst, 1)
            dve.wait_ge(s.mst, 2)
            tt(mast[:, :, 0], mast[:, :, 1], cnt[:, :, 1], ALU.mult).then_inc(s.mst, 1)
            dve.wait_ge(s.mst, 3)
            tt(feats[:, :, 2], mast[:, :, 0], ok, ALU.mult).then_inc(s.feats_ok, 1)
            wait_full(dve, "small")
            tt(k10[:], bc_mid(at("small")[:, 0:2 * FEAT], GT), bc(own_quarter[:], 2 * FEAT), ALU.mult).then_inc(s.k10_ok, 1)
            tt(wc_blk[:], bc_mid(at("small")[:, 64:128], 8), bc(own_block[:], C), ALU.mult).then_inc(s.wcblk_ok, 1)
            read(tt(w16_blk[:], bc_mid(at("small")[:, 128:192], 8), bc(own_block[:], C), ALU.mult), "small")
            dve.wait_ge(s.proj_hi, 1)
            tt(qkv_l[:], qkv_s[:], qkv_h[:].bitcast(F32), ALU.subtract)
            tt(rt_l[:], rt_s[:], rt_h[:].bitcast(F32), ALU.subtract).then_inc(s.proj_lo, 1)
            for k in range(2):
                wait_read(dve, f"hc{k}")
            dve.tensor_reduce(var0[:], hsq, AX.X, ALU.add).then_inc(s.var0_ok, 1)
            dve.wait_ge(s.inv0_ok, 2)
            tt(g5[:, :, 0:4], feats[:, :, 0:4], bc(inv0[:], 4), ALU.mult)
            dve.memset(g5[:, :, 4:5], 1.0).then_inc(s.g5_ok, 1)
            dve.wait_ge(s.g5_ok, 1)
            dve.tensor_copy(feats[:, :, 4:8], g5[:, :, 0:4])
            wait_full(dve, "z")
            for k in range(2):
                ins = dve.tensor_copy(z[:, k, :, 0:FEAT],
                                      at("z")[:, 32:32 + 2 * FEAT * NB].rearrange("p (b c) -> p b c", b=NB)[:, :, FEAT * k:FEAT * k + FEAT])
            read(ins, "z")
            wait_read(dve, "z")
            wait_full(dve, "gsum")
            read(tt(zg[:], z[:, 0, :, 0:FEAT], at("gsum")[:, 0:FEAT * NB].rearrange("p (b c) -> p b c", b=NB), ALU.mult), "gsum")
            wait_read(dve, "gsum")
            dve.tensor_reduce(score[:], zg[:], AX.X, ALU.add).then_inc(s.score_ok, 1)
            wait_full(dve, "scT")
            read(dve.tensor_copy(score_T[:, 0], at("scT")[0:NB, 0:P]), "scT")
            wait_read(dve, "scT")
            for k in range(5):
                dve.max(top8[:, k], score_T[:, k]).then_inc(s.topk, 1)
                dve.wait_ge(s.topk, 2 * k + 1)
                dve.match_replace(score_T[:, k + 1], top8[:, k], score_T[:, k], NEG).then_inc(s.topk, 1)
                dve.wait_ge(s.topk, 2 * k + 2)
            dve.tensor_scalar(chosen[:], score_T[:, 5], NEG, None, ALU.is_equal).then_inc(s.chosen_ok, 1)
            dve.memset(ones16[:], 1.0).then_inc(s.chosen_ok, 1)
            dve.wait_ge(s.chosen_ok, 2)
            dve.tensor_tensor_scan(count_T[:], ones16[:], chosen[:], 0.0, ALU.mult, ALU.add).then_inc(s.count_ok, 1)
            dve.wait_ge(s.count_ok, 1)
            tt(place_T[:], count_T[:], chosen[:], ALU.mult).then_inc(s.place_ok, 1)
            wait_full(dve, "posT")
            read(tt(pick, bc_mid(rank_iota[:], NB), bc(at("posT")[:, 0:NB], LAND), ALU.is_equal), "posT")
            for k in range(4):
                lg = at(("logit", k))[:, 0:GT * 2 * LAND].rearrange("p (r l) -> p r l", l=LAND)
                wait_full(dve, ("logit", k))
                dve.tensor_reduce(lmax[:, k], lg, AX.X, ALU.max).then_inc(s.lmax_ok, 1)
                dve.wait_ge(s.lmax_ok, k + 1)
                read(tt(lsub[:, k], lg, bc(lmax[:, k], LAND), ALU.subtract), ("logit", k))
            dve.wait_ge(s.eexp, 1)
            dve.tensor_reduce(lsum[:, 0], eq[:, :, 0:LAND], AX.X, ALU.add)
            dve.tensor_reduce(lsum[:, 1], ek, AX.X, ALU.add).then_inc(s.lsum_ok, 1)
            dve.wait_ge(s.lsum_ok, 1)
            dve.reciprocal(linv[:].rearrange("p a b -> p (a b)"), lsum[:].rearrange("p a b -> p (a b)")).then_inc(s.linv_ok, 1)
            dve.wait_ge(s.linv_ok, 1)
            tt(g5k[:], g5[:, :, 0:FEAT], bc(linv[:, 1], FEAT), ALU.mult).then_inc(s.g5k_ok, 1)
            wait_full(dve, "gb")
            for r in range(2):
                ins = dve.tensor_copy(gsum_l[64 * r:64 * r + LAND, :, r],
                                      at("gb")[64 * r:64 * r + LAND, 32:32 + 8 * FEAT].rearrange("p (a b) -> p a b", b=FEAT))
            read(ins, "gb")
            wait_full(dve, "a")
            read(tt(feats[:, :, 8:13], at("a")[:, 0:NB * FEAT].rearrange("p (b c) -> p b c", b=NB), bc(linv[:, 0], FEAT),
                    ALU.mult), "a")
            dve.memset(feats[:, :, 13:14], 1.0).then_inc(s.attended, 1)
            for k in range(2):
                part = slice(k * NCH * P, (k + 1) * NCH * P)
                dve.wait_ge(s.w13_hi, k + 1)
                tt(w13_l[:, part], w13_raw[:, part], w13_h[:, part].bitcast(F32), ALU.subtract).then_inc(s.w13_lo, 1)
            dve.wait_ge(s.ew_hi, 1)
            tt(ew_l[:], mix_w[:, 0:32 + NE1 * C], ew_h[:].bitcast(F32), ALU.subtract)
            dve.wait_ge(s.b3_hi, 1)
            dve.tensor_copy(b3_hl[0:1, :], b3_raw[0:1, :])
            tt(b3_hl[32:33, :], b3_raw[32:33, :], b3_h[32:33, :].bitcast(F32), ALU.subtract).then_inc(s.ew_lo, 1)
            wait_full(dve, ("h1", 0))
            read(dve.tensor_copy(h1[:, 0:8].rearrange("p a b -> p (a b)"), at(("h1", 0))[:]), ("h1", 0))

            def centre(n, g, src):
                t = centre_turn[n, g]
                dve.tensor_reduce(nsum[n][g], src, AX.X, ALU.add).then_inc(s.nsum_ok, 1)
                dve.wait_ge(s.nsum_ok, t)
                dve.scalar_tensor_tensor(out=ncen[n][g], in0=bc(nsum[n][g], C), scalar=-1.0 / C, in1=src,
                                         op0=ALU.mult, op1=ALU.add).then_inc(s.ncen_ok, 1)

            def sum_squares(n, g):
                dve.wait_ge(s.nsq_ok, norm_turn[n, g])
                dve.tensor_reduce(nss[n][g], nsq[n][g], AX.X, ALU.add).then_inc(s.nss_ok, 1)

            def scaled(n, g, src, row):
                dve.wait_ge(s.ninv_ok, inv_turn[n, g])
                tt(xs[split_of[n]][g], src, bc(ninv[n][g][:, row], C), ALU.mult).then_inc(s.xs_ok, 1)

            def lo_part(n, g):
                k = split_of[n]
                dve.wait_ge(s.xhi_ok, split_turn[n, g])
                tt(xhl[k][g][:, :, 1], xs[k][g], xhl[k][g][:, :, 0].bitcast(F32), ALU.subtract).then_inc(s.xlo_ok, 1)

            def route(lay, g, key, r, e):
                count = (s.router0, s.router1)[lay]
                place = [ROUTER_OPS * g]

                def link(ins):
                    place[0] += 1
                    ins.then_inc(count, 1)
                    dve.wait_ge(count, place[0])

                wait_full(dve, key)
                lg = at(key)[:, 0:GT * e].rearrange("p (t e) -> p t e", e=e)
                link(dve.tensor_reduce(r.lmax[g], lg, AX.X, ALU.max))
                read(tt(r.lsub[g], lg, bc(r.lmax[g], e), ALU.subtract), key)
                if lay:
                    dve.wait_ge(s.route_exp1, 2 * g + 1)
                else:
                    dve.wait_ge(s.route_exp0, g + 1)
                link(dve.tensor_reduce(r.s[g], r.ex[g], AX.X, ALU.add))
                link(dve.reciprocal(r.inv[g], r.s[g]))
                link(tt(r.p[g], r.ex[g], bc(r.inv[g], e), ALU.mult))
                link(tt(r.eq1[g], r.p[g], bc(r.inv[g], e), ALU.is_equal))
                link(tt(r.key1[g], r.eq1[g], bc_mid(rev_iota[:, 0:e], GT), ALU.mult))
                link(dve.tensor_reduce(r.best1[g], r.key1[g], AX.X, ALU.max))
                link(tt(r.one1[g], r.key1[g], bc(r.best1[g], e), ALU.is_equal))
                link(dve.scalar_tensor_tensor(out=r.rest[g], in0=r.one1[g], scalar=-4.0, in1=r.p[g], op0=ALU.mult, op1=ALU.add))
                link(dve.tensor_reduce(r.max2[g], r.rest[g], AX.X, ALU.max))
                link(tt(r.eq2[g], r.rest[g], bc(r.max2[g], e), ALU.is_equal))
                link(tt(r.key2[g], r.eq2[g], bc_mid(rev_iota[:, 0:e], GT), ALU.mult))
                link(dve.tensor_reduce(r.best2[g], r.key2[g], AX.X, ALU.max))
                link(tt(r.one2[g], r.key2[g], bc(r.best2[g], e), ALU.is_equal))
                if lay:
                    link(tt(r.sub2[g], r.p[g], bc(r.inv[g], e), ALU.subtract))
                    link(tt(r.both[g], r.one1[g], r.one2[g], ALU.add))
                    dve.wait_ge(s.route_exp1, 2 * g + 2)
                    link(tt(r.pw[g], r.ex2[g], r.both[g], ALU.mult))
                    link(dve.tensor_reduce(r.den[g], r.pw[g], AX.X, ALU.add))
                else:
                    link(tt(r.both[g], r.one1[g], r.one2[g], ALU.add))
                    link(tt(r.pw[g], r.p[g], r.both[g], ALU.mult))
                    link(dve.tensor_reduce(r.sum2[g], r.pw[g], AX.X, ALU.add))
                    link(dve.tensor_scalar(r.den[g], r.sum2[g], 1e-9, None, ALU.add))
                link(dve.reciprocal(r.deni[g], r.den[g]))
                link(tt(r.w[g], r.pw[g], bc(r.deni[g], e), ALU.mult))
                assert place[0] == ROUTER_OPS * (g + 1)

            def weigh(q, j):
                wait_full(dve, ("pair", q, j))
                if q >= 1:
                    dve.wait_ge(s.acc0_ok, 3 * (q - 1) + max(j, 1))
                read(tt(weighted[j], at(("pair", q, j))[:].rearrange("p (t e c) -> p t e c", t=GT, e=2),
                        bc(rs[0].w[q][:, :, 2 * j:2 * j + 2], C), ALU.mult), ("pair", q, j))

            def finish(q):
                dve.wait_ge(s.acc0_ok, 3 * (q + 1))
                tt(folded[q], acc[q][:, :, 0], acc[q][:, :, 1], ALU.add).then_inc(s.fold0_ok, 1)
                dve.wait_ge(s.fold0_ok, q + 1)
                dve.wait_ge(s.h12_ok, q + 1)
                tt(grp(h2, q), folded[q], grp(h12, q), ALU.add).then_inc(s.h2_ok, 1)

            def weigh1(g, c):
                wait_full(dve, ("oc", g, c))
                if g >= 1:
                    dve.wait_ge(s.acc1_ok, 2 * (g - 1) + max(c, 1))
                read(tt(weighted1[c], at(("oc", g, c))[:].rearrange("p (t e c) -> p t e c", t=GT, e=2),
                        bc(rs[1].w[g][:, :, 2 * c:2 * c + 2], C), ALU.mult), ("oc", g, c))

            for step, g in ORDER:
                if step == "F0":
                    if g == 0:
                        for k in range(2):
                            wait_read(dve, ("h1", k))
                    centre(0, g, grp(h1, g))
                    sum_squares(0, g)
                    scaled(0, g, ncen[0][g], 1)
                    tt(x2[g], ncen[0][g], bc(ninv[0][g][:, 0], C), ALU.mult).then_inc(s.x2_ok, 1)
                    lo_part(0, g)
                elif step == "F1":
                    dve.wait_ge(bank_free[bank["qkv", g]], done["qkv", g] - 1)
                    qk = at(("qkv", g))[:].rearrange("p (t h d) -> p t h d", t=GT, d=HD)[:, :, 0:6]
                    cos = bc_mid(bc_mid(ffnp("cos"), 6), GT)
                    sin = bc_mid(bc_mid(ffnp("sin"), 6), GT)
                    hh = HD // 2
                    tt(rope1[g], qk, cos, ALU.mult)
                    tt(rope2[g][:, :, :, 0:hh], qk[:, :, :, hh:HD], sin[:, :, :, 0:hh], ALU.mult)
                    read(tt(rope2[g][:, :, :, hh:HD], qk[:, :, :, 0:hh], sin[:, :, :, hh:HD], ALU.mult), ("qkv", g))
                    wait_full(dve, ("kT", g))
                    if g >= 2:
                        dve.wait_ge(s.pv_done, GT * (g - 1))
                    read(dve.tensor_copy(kT[g % 2][:].rearrange("p a b -> p (a b)"), at(("kT", g))[:]), ("kT", g))
                elif step == "F2":
                    for i in range(GT):
                        t = GT * g + i
                        wait_full(dve, ("s", g, i))
                        sc = at(("s", g, i))[:].rearrange("p (t s) -> p t s", t=GT)
                        dve.tensor_reduce(smax[g][:, i], sc, AX.X, ALU.max).then_inc(s.smax_ok, 1)
                        dve.wait_ge(s.smax_ok, t + 1)
                        if t >= 4:
                            dve.wait_ge(s.sexp_ok, t - 3)
                        read(tt(probs[t % 4], sc, bc(smax[g][:, i], P), ALU.subtract), ("s", g, i))
                    dve.wait_ge(s.pv_done, GT * (g + 1))
                    yy = at(("y", g))[:, 0:GT * NH * (HD + 1)].rearrange("p (r d) -> p r d", d=HD + 1)
                    dve.reciprocal(yinv[g], yy[:, :, HD]).then_inc(s.yinv_ok, 1)
                    dve.wait_ge(s.yinv_ok, g + 1)
                    read(tt(ynorm[g].rearrange("p t (h d) -> p (t h) d", h=NH), yy[:, :, 0:HD], bc(yinv[g], HD), ALU.mult),
                         ("y", g))
                elif step == "F3":
                    wait_full(dve, ("proj", g))
                    dve.wait_ge(s.x2_ok, g + 1)
                    read(tt(xres[g], at(("proj", g))[:, 0:GT * C].rearrange("p (t c) -> p t c", t=GT), x2[g], ALU.add),
                         ("proj", g))
                    sum_squares(1, g)
                elif step == "F4":
                    scaled(1, g, xres[g], 0)
                    lo_part(1, g)
                    route(0, g, ("route", g), rs[0], NE0)
                elif step == "M0":
                    for t in range(NG * NCH + 2):
                        q, n = divmod(t, NCH)
                        if t < NG * NCH:
                            if q >= 1:
                                wait_full(dve, ("pair", q - 1, LAST_PAIR[n]))
                            wait_full(dve, ("u3", t))
                            wait_read(dve, ("u1", t))
                            tt(hid[n], at(("u3", t))[:], gate[t % 3], ALU.mult).then_inc(s.hid_ok, 1)
                        if t >= 2 and (t - 2) % NCH in PAIR_AFTER:
                            j = PAIR_AFTER.index((t - 2) % NCH)
                            weigh((t - 2) // NCH, j)
                            if j == 0 and t >= NCH:
                                finish((t - 2) // NCH - 1)
                    finish(NG - 1)
                elif step == "A1":
                    dve.wait_ge(s.h2_ok, g + 1)
                    centre(2, g, grp(h2, g))
                    sum_squares(2, g)
                    dve.wait_ge(s.ninv_ok, inv_turn[2, g])
                    tt(x3[g], ncen[2][g], bc(ninv[2][g][:, 0], C), ALU.mult).then_inc(s.x3_ok, 1)
                elif step == "A2":
                    wait_full(dve, ("sim", g))
                    sm = at(("sim", g))[:].rearrange("p (t s) -> p t s", t=GT)
                    dve.tensor_reduce(m1[g], sm, AX.X, ALU.max).then_inc(s.m1_ok, 1)
                    dve.wait_ge(s.m1_ok, g + 1)
                    if g >= 2:
                        dve.wait_ge(s.e1_ok, g - 1)
                    read(tt(p1[g % 2], sm, bc(m1[g], P), ALU.subtract), ("sim", g))
                    wait_full(dve, ("o1", g))
                    oo = at(("o1", g))[:, 0:GT * C].rearrange("p (t c) -> p t c", t=GT)
                    dve.reciprocal(o1inv[g], at(("o1", g))[:, GT * C:GT * C + GT]).then_inc(s.o1inv_ok, 1)
                    dve.wait_ge(s.o1inv_ok, g + 1)
                    read(tt(o1[g], oo, bc(o1inv[g], C), ALU.mult), ("o1", g))
                elif step == "M1":
                    dve.wait_ge(s.h3_ok, g + 1)
                    centre(3, g, grp(h3, g))
                    sum_squares(3, g)
                    scaled(3, g, ncen[3][g], 0)
                    lo_part(3, g)
                    route(1, g, ("route1", g), rs[1], NE1)
                elif step == "M2":
                    for c in range(3):
                        wait_full(dve, ("h2c", g, c))
                        t = 3 * g + c
                        if t >= 2:
                            wait_full(dve, ("oc",) + divmod(t - 2, 3))
                        read(dve.tensor_scalar(hid2[t % 2], at(("h2c", g, c))[:], mixp("eb2")[:, c:c + 1], 0.0, ALU.add,
                                               ALU.max), ("h2c", g, c))
                        if c >= 1:
                            weigh1(g, c - 1)
                    weigh1(g, 2)
                    dve.wait_ge(s.acc1_ok, 2 * (g + 1))
                    tt(folded[g], acc1[g][:, :, 0], acc1[g][:, :, 1], ALU.add).then_inc(s.fold1_ok, 1)
                    dve.wait_ge(s.fold1_ok, g + 1)
                    tt(grp(h4, g), folded[g], grp(h3, g), ALU.add).then_inc(s.h4_ok, 1)

        @block.tensor
        def _(pe):
            def mm(o, l, r, start=True, stop=True, **kw):
                return pe.matmul(o, l, r, start=start, stop=stop, skip_group_check=True)

            def rows_out(o, x, wh, wl, start=True):
                mm(o, x, wh, start=start)
                return mm(o, x, wl, start=False)

            def columns_out(o, wh, wl, x):
                mm(o, wh, x)
                return mm(o, wl, x, start=False)

            pe.wait_ge(s.p1c_ok, 3)
            a, _b = TOK_PARTS["augb"]
            written(mm(at("mct")[0:C, 0:4], p1c[:], tok_w[0:C + 1, a + 4:a + 8]), "mct")
            wait_read(pe, "mct")
            pe.wait_ge(s.attw_in, 16)
            for n, w in enumerate(("wqT", "wkT", "wvT")):
                ins = mm(at("qkv5")[0:C, 8 * n:8 * n + 4], attp(w), mct[:], start=(n == 0))
            written(ins, "qkv5")
            pe.wait_ge(s.one_r_ok, 2)
            for b in range(NB):
                pe.wait_ge(s.same_ok, b + 1)
                ins = mm(at("cnt")[:, 2 * b:2 * b + 2], same[:, b], one_r[:, b], start=(b == 0))
            written(ins, "cnt")
            wait_read(pe, "qkv5")
            sm = at("small")
            mm(sm[:, 64:128], tokp("auga", C + 1), p1c[:])
            mm(sm[:, 0:2 * FEAT], k5_pad[:].rearrange("p a b -> p (a b)"), qk5[:], start=False)
            mm(sm[:, 128:192], tokp("auga"), tokp("p1"), start=False)
            mm(sm[:, 128:192], tokp("augb", C + 1), p1c[:], start=False)
            written(mm(sm[:, 128:192], v5_pad[:].rearrange("p a b -> p (a b)"), attp("woT"), start=False), "small")
            pe.wait_ge(s.feats_ok, 1)
            for k in range(2):
                ins = pe.transpose(at("ut0")[:, P * k:P * k + P], feats[:, 8 * k:8 * k + 8].rearrange("p a b -> p (a b)"), ident[:])
            written(ins, "ut0")
            wait_read(pe, "ut0")
            pe.wait_ge(s.wcblk_ok, 1)
            for k in range(2):
                written(mm(at(f"hc{k}")[:], feats_T[:, k], wc_blk[:].rearrange("p a b -> p (a b)")), f"hc{k}")
            pe.wait_ge(s.g5_ok, 1)
            for k in range(4):
                ins = pe.transpose(at("gT")[:, P * k:P * k + P], g5[:, GT * k:GT * k + GT].rearrange("p a b -> p (a b)"), ident[:])
            written(ins, "gT")
            wait_free(pe, "gsum")
            written(mm(at("gsum")[:, 0:FEAT * NB], ones[:], g5[:, :, 0:FEAT]), "gsum")
            wait_free(pe, "z")
            wait_read(pe, "gT")
            pe.wait_ge(s.k10_ok, 1)
            for q in range(NG):
                w = GT * 2 * FEAT
                ins = mm(at("z")[:, 32 + w * q:32 + w * (q + 1)], g5_T[:, q], k10[:].rearrange("p a b -> p (a b)"), start=(q == 0))
            written(ins, "z")
            pe.wait_ge(s.score_ok, 1)
            wait_free(pe, "scT")
            written(pe.transpose(at("scT")[0:NB, 0:P], score[:], ident[:]), "scT")
            pe.wait_ge(s.place_ok, 1)
            wait_free(pe, "posT")
            written(pe.transpose(at("posT")[:, 0:NB], place_T[:], ident[0:NB, 0:NB]), "posT")
            wait_free(pe, "landq")
            wait_read(pe, "posT")
            for b in range(NB):
                r = 32 * (b % GT)
                for k in range(2):
                    c0 = 16 + 2 * LAND * (b // GT) + LAND * k
                    ins = mm(at("landq")[r:r + 32, c0:c0 + LAND], z[:, k, b], pick[:, b])
            written(ins, "landq")
            wait_read(pe, "landq")
            for i in range(GT):
                wait_free(pe, ("logit", i))
                for q in range(NG):
                    ins = mm(at(("logit", i))[:, 2 * LAND * q:2 * LAND * (q + 1)], g5_T[32 * i:32 * i + 32, q],
                             y10[32 * i:32 * i + 32, q], start=(q == 0))
                written(ins, ("logit", i))
            pe.wait_ge(s.g5k_ok, 1)
            wait_free(pe, "gb")
            for b in range(NB):
                r = 64 * (b % 2)
                ins = mm(at("gb")[r:r + LAND, 32 + FEAT * (b // 2):32 + FEAT * (b // 2 + 1)], ek[:, b], g5k[:, b], start=(b < 2))
            written(ins, "gb")
            for k in range(2):
                wait_free(pe, ("eqT", k))
                for j in range(4):
                    b = 8 * k + 2 * j
                    ins = pe.transpose(at(("eqT", k))[:, P * j:P * j + P], eq[:, b:b + 2].rearrange("p a b -> p (a b)"), ident[:])
                written(ins, ("eqT", k))
            wait_read(pe, "gb")
            for k in range(2):
                wait_read(pe, ("eqT", k))
            wait_free(pe, "a")
            for b in range(0, NB, 2):
                ins = mm(at("a")[:, FEAT * b:FEAT * (b + 2)], eq_T[:, b // 2], gsum_l[:, b // 2].rearrange("p a b -> p (a b)"),
                         start=(b == 0))
            written(ins, "a")
            pe.wait_ge(s.attended, 1)
            wait_read(pe, "a")
            wait_free(pe, "ut1")
            for k in range(2):
                ins = pe.transpose(at("ut1")[:, P * k:P * k + P], feats[:, 8 * k:8 * k + 8].rearrange("p a b -> p (a b)"), ident[:])
            written(ins, "ut1")
            wait_read(pe, "ut1")
            for k in range(2):
                wait_free(pe, ("h1", k))
                written(mm(at(("h1", k))[:], feats_T1[:, k], w16_blk[:].rearrange("p a b -> p (a b)")), ("h1", k))
            wait_free(pe, "l1a")
            written(mm(at("l1a")[:, 0:C], attp("l1wq"), attp("l1wk")), "l1a")

            def stack_T(n, g, key):
                pe.wait_ge(s.xlo_ok, split_turn[n, g])
                wait_free(pe, key)
                for i in range(GT):
                    ins = pe.transpose(at(key)[:, P * i:P * i + P],
                                       xhl[split_of[n]][g][:, i].rearrange("p a b -> p (a b)").bitcast(F32), ident[:])
                written(ins, key)

            for step, g in ORDER:
                if step == "F0":
                    stack_T(0, g, ("xt", g))
                    wait_read(pe, ("xt", g))
                    wait_free(pe, ("qkv", g))
                    if g == 0:
                        pe.wait_ge(s.proj_lo, 1)
                    for i in range(GT):
                        ins = rows_out(at(("qkv", g))[:, P * i:P * i + P], xT[0][g][:, i], qkv_h[:], qkv_l[:], start=(i == 0))
                    written(ins, ("qkv", g))
                elif step == "F1":
                    pe.wait_ge(s.qkpad_ok, g + 1)
                    for key, src in ((("qT", g), q_pad[g % 2][:].rearrange("p t h d -> p t (h d)")),
                                     (("kT", g), k_pad[g % 2][:].rearrange("p t k r d -> p t (k r d)"))):
                        wait_free(pe, key)
                        for i in range(GT):
                            ins = pe.transpose(at(key)[:, P * i:P * i + P], src[:, i], ident[:])
                        written(ins, key)
                elif step == "F2":
                    if g == 0:
                        pe.wait_ge(s.const, CONST_ALL)
                    wait_read(pe, ("qT", g))
                    wait_read(pe, ("kT", g))
                    for i in range(GT + 2):
                        if i < GT:
                            key = ("s", g, i)
                            wait_free(pe, key)
                            mm(at(key)[:], ident_b[:], neg_mask[:].rearrange("p a b -> p (a b)"))
                            for b in range(GT):
                                ins = mm(at(key)[:, P * b:P * b + P], qT[g % 2][32 * i:32 * i + HD, b],
                                         kT[g % 2][32 * i:32 * i + HD, b], start=False)
                            written(ins, key)
                        if 1 <= i <= GT:
                            key, t = ("pT", g, i - 1), GT * g + i - 1
                            pe.wait_ge(s.sexp_ok, t + 1)
                            wait_free(pe, key)
                            for b in range(GT):
                                ins = pe.transpose(at(key)[:, P * b:P * b + P], expd[t % 4][:, b], ident[:])
                            written(ins, key)
                        if i >= 2:
                            key, t = ("pT", g, i - 2), GT * g + i - 2
                            wait_read(pe, key)
                            if i == 2:
                                wait_free(pe, ("y", g))
                            w = HD + 1
                            for b in range(GT):
                                r = NH * b + i - 2
                                ins = mm(at(("y", g))[:, w * r:w * r + w], probs_T[t % 4][:, b], v1[g][:, b, (i - 2) // 2],
                                         start=(r == 0))
                            ins.then_inc(s.pv_done, 1)
                elif step == "F3":
                    wait_free(pe, ("yT", g))
                    wait_read(pe, ("y", g))
                    for i in range(2):
                        ins = pe.transpose(at(("yT", g))[:, P * i:P * i + P], ynorm[g][:, 2 * i:2 * i + 2].rearrange("p a b -> p (a b)"),
                                           ident[:])
                    written(ins, ("yT", g))
                    wait_read(pe, ("yT", g))
                    wait_free(pe, ("proj", g))
                    for i in range(2):
                        ins = mm(at(("proj", g))[:, P * i:P * i + P], yT[g][:, i], ffnp("wo"), start=(i == 0))
                    written(ins, ("proj", g))
                elif step == "F4":
                    stack_T(1, g, ("xt2", g))
                    wait_read(pe, ("xt2", g))
                    wait_free(pe, ("route", g))
                    for i in range(GT):
                        ins = rows_out(at(("route", g))[:, NE0 * i:NE0 * i + NE0], xT[1][g][:, i], rt_h[:], rt_l[:], start=(i == 0))
                    written(ins, ("route", g))
                elif step == "M0":
                    pe.wait_ge(s.w13_lo, 2)
                    pe.wait_ge(s.w2_in, 16)

                    def pair(q, j):
                        key = ("pair", q, j)
                        wait_free(pe, key)
                        for i in range(GT):
                            tile = slice(P * i, P * i + P)
                            base = 2 * C * i
                            for m in range(2):
                                e = 2 * j + m
                                mm(at(key)[:, base + C * m:base + C * m + C], hid[CHUNK_AT["f", e]][:, tile],
                                   w2_sb[:, C * e:C * e + C], start=(i == 0 and m == 0))
                            for n in sorted({(2 * j) // 3, (2 * j + 1) // 3}):
                                es = [e for e in (2 * j, 2 * j + 1) if e // 3 == n]
                                lo = base + C * (es[0] - 2 * j)
                                ins = mm(at(key)[:, lo:lo + C * len(es)], hid[CHUNK_AT["r", n]][:, tile],
                                         w2_sb[:, 512 + C * es[0]:512 + C * (es[-1] + 1)], start=False)
                        written(ins, key)

                    for t in range(NG * NCH + 1):
                        q, n = divmod(t, NCH)
                        if t < NG * NCH:
                            x = xT[1][q].rearrange("p a b -> p (a b)")
                            for u, off in (("u1", 0), ("u3", NCH * P)):
                                key = (u, t)
                                wait_free(pe, key)
                                if u == "u3" and t >= 2:
                                    pe.wait_ge(s.hid_ok, t - 1)
                                cols = slice(off + P * n, off + P * n + P)
                                written(columns_out(at(key)[:], w13_h[:, cols], w13_l[:, cols], x), key)
                        if t and (t - 1) % NCH in PAIR_AFTER:
                            pe.wait_ge(s.hid_ok, t)
                            pair((t - 1) // NCH, PAIR_AFTER.index((t - 1) % NCH))
                elif step == "A1":
                    key = ("x3T", g)
                    pe.wait_ge(s.x3_ok, g + 1)
                    wait_free(pe, key)
                    for i in range(2):
                        ins = pe.transpose(at(key)[:, P * i:P * i + P], x3[g][:, 2 * i:2 * i + 2].rearrange("p t c -> p (t c)"), ident[:])
                    written(ins, key)
                    wait_read(pe, key)
                    if g == 0:
                        wait_read(pe, "l1a")
                    wait_free(pe, ("u", g))
                    for r in (0, C):
                        ins = mm(at(("u", g))[r:r + C, 0:2 * P], l1a[r:r + C, :], x3T[g][r:r + C].rearrange("p a b -> p (a b)"))
                    written(ins, ("u", g))
                    wait_read(pe, ("u", g))
                    wait_free(pe, ("sim", g))
                    for i in (0, 2, 1, 3):
                        r = C * (i % 2)
                        if i == 1:
                            pe.wait_ge(s.sim_half, g + 1)
                        ins = mm(at(("sim", g))[:, P * i:P * i + P], uT[g][r:r + C, i // 2], x3T[g][r:r + C, i // 2], start=(i == 0))
                        if i == 2:
                            ins.then_inc(s.sim_half, 1)
                    written(ins, ("sim", g))
                elif step == "A2":
                    key = ("p1T", g)
                    pe.wait_ge(s.e1_ok, g + 1)
                    wait_free(pe, key)
                    for i in range(GT):
                        ins = pe.transpose(at(key)[:, P * i:P * i + P], e1[g % 2][:, i], ident[:])
                    written(ins, key)
                    wait_read(pe, key)
                    wait_free(pe, ("o1", g))
                    for i in range(GT):
                        mm(at(("o1", g))[:, C * i:C * i + C], p1T[g % 2][:, i], x3[g][:, i], start=(i == 0))
                        ins = mm(at(("o1", g))[:, GT * C + i:GT * C + i + 1], p1T[g % 2][:, i], ones[:, 0:1], start=False)
                    written(ins, ("o1", g))
                elif step == "M1":
                    stack_T(3, g, ("xt3", g))
                    wait_read(pe, ("xt3", g))
                    x = xT[2][g].rearrange("p a b -> p (a b)")
                    if g == 0:
                        pe.wait_ge(s.ew_lo, 1)
                    wait_free(pe, ("rh", g))
                    written(columns_out(at(("rh", g))[0:32, :], ew_h[:, 0:32], ew_l[:, 0:32], x), ("rh", g))
                    wait_read(pe, ("rh", g))
                    for i in range(GT):
                        ins = mm(at(("route1", g))[:, NE1 * i:NE1 * i + NE1], rh[g][:, P * i:P * i + P], mixp("rw2", 33), start=(i == 0))
                    written(ins, ("route1", g))
                elif step == "M2":
                    x = xT[2][g].rearrange("p a b -> p (a b)")

                    def layer1(c):
                        key = ("h1c", g, c)
                        wait_free(pe, key)
                        cols = slice(32 + P * c, 32 + P * c + P)
                        written(columns_out(at(key)[:], ew_h[:, cols], ew_l[:, cols], x), key)

                    layer1(0)
                    for c in range(3):
                        t = 3 * g + c
                        wait_read(pe, ("h1c", g, c))
                        if c < 2:
                            layer1(c + 1)
                        key = ("h2c", g, c)
                        wait_free(pe, key)
                        written(mm(at(key)[:], mixp("ew2")[:, P * c:P * c + P], hid1[t % 2]), key)
                        wait_read(pe, key)
                        key = ("oc", g, c)
                        wait_free(pe, key)
                        mm(at(key)[:], ones33[:], bc_mid(b3_hl[:, P * c:P * c + P], GT))
                        for i in range(GT):
                            ins = mm(at(key)[:, P * i:P * i + P], hid2[t % 2][:, P * i:P * i + P], mixp("ew3")[:, P * c:P * c + P],
                                     start=False)
                        written(ins, key)



def kernel(**inputs):
    import numpy as _np
    import concourse.bacc as _bacc
    from concourse.bass_utils import run_bass_kernel_spmd as _run

    a = {k: _np.asarray(v) for k, v in inputs.items()}
    f32 = _np.float32

    def place(parts, width, rows, pieces):
        whole = _np.zeros((rows, width), f32)
        for name, piece in pieces.items():
            lo, hi = parts[name]
            whole[:piece.shape[0], lo:hi] = piece
        return whole

    def col(v):
        return v.reshape(-1, 1)

    def twice(m):
        return _np.concatenate([m, m], axis=0)

    d3 = a["L0_tok_skill_w"].shape[0]
    p1 = _np.concatenate([a["L0_tok_proj_w"].T, a["L0_tok_proj_b"][None], a["L0_attn_bo"][None]], axis=0)
    feat = _np.zeros((C + 2, 4), f32)
    feat[0:d3, 0] = a["L0_tok_skill_w"]
    feat[d3:2 * d3, 1] = a["L0_tok_att_w"]
    feat[2 * d3:C, 2] = a["L0_tok_mast_w"]
    feat[0:d3, 3] = a["L0_tok_skill_b"]
    feat[d3:2 * d3, 3] = a["L0_tok_att_b"]
    feat[2 * d3:C, 3] = a["L0_tok_mast_b"]
    feat[C, 3] = 1
    auga = _np.zeros((C + 2, 8, 16), f32)
    augb = _np.zeros((C + 2, 8, 16), f32)
    auga[:, :, 0:4] = feat[:, None, :]
    augb[:, :, 4:8] = feat[:, None, :]
    auga[C + 1, :, 13] = 1
    tokw = place(TOK_PARTS, TOK_W, C + 2, {"p1": p1, "auga": auga.reshape(C + 2, P), "augb": augb.reshape(C + 2, P)})

    attw = place(ATT_PARTS, ATT_W, C, {
        "wqT": a["L0_attn_Wq"].T, "wkT": a["L0_attn_Wk"].T, "wvT": a["L0_attn_Wv"].T, "woT": a["L0_attn_Wo"].T,
        "bq": col(a["L0_attn_bq"]), "bk": col(a["L0_attn_bk"]), "bv": col(a["L0_attn_bv"]),
        "l1wq": _np.concatenate([a["L1_attn_Wq"], a["L1_attn_Wq"]], axis=1), "l1wk": a["L1_attn_Wk"]})

    freq = 1.0 / 10000.0 ** (_np.arange(0, HD, 2, dtype=f32) / HD)
    angle = _np.outer(_np.arange(P, dtype=f32), freq)
    cos, sin = _np.cos(angle).astype(f32), _np.sin(angle).astype(f32)
    wo = _np.zeros((2, C, 2, C), f32)
    wo[0, :, 0] = wo[1, :, 1] = a["L0_ffn_wo"].T
    wo = wo.reshape(P, 2 * C)
    ffnw = place(FFN_PARTS, FFN_W, P, {
        "wqkv": twice(_np.concatenate([a["L0_ffn_wq"].T, a["L0_ffn_wk"].T, a["L0_ffn_wv"].T], axis=1)),
        "wo": wo, "router": twice(a["L0_ffn_router_w"].T),
        "ln1": twice(col(a["L0_ffn_ln1_w"])), "ln2": twice(col(a["L0_ffn_ln2_w"])),
        "cos": _np.concatenate([cos, cos], axis=1), "sin": _np.concatenate([-sin, sin], axis=1)})

    w13 = _np.zeros((C, 2, NCH, P), f32)
    for k, w in enumerate((a["L0_ffn_w1"], a["L0_ffn_w3"])):
        for n, (kind, m) in enumerate(CHUNKS):
            if kind == "f":
                w13[:, k, n] = w[m, 0:P].T
            else:
                for i, e in enumerate(range(3 * m, min(3 * m + 3, NE0))):
                    w13[:, k, n, REM * i:REM * i + REM] = w[e, P:HID].T
    w13 = twice(w13.reshape(C, 2 * NCH * P))
    w2 = _np.zeros((P, 2, NE0, C), f32)
    for e in range(NE0):
        w2[:, 0, e] = a["L0_ffn_w2"][e, :, 0:P].T
        w2[REM * (e % 3):REM * (e % 3) + REM, 1, e] = a["L0_ffn_w2"][e, :, P:HID].T
    w2 = w2.reshape(P, 2 * NE0 * C)

    def diagonal(w):
        blocks = _np.zeros((2, C, 3, 2, C), f32)
        for e in range(NE1):
            blocks[e % 2, :, e // 2, e % 2] = w[e]
        return blocks.reshape(P, NE1 * C)

    def by_pairs(b):
        return _np.ascontiguousarray(b.reshape(3, P).T)

    mixw = place(MIX_PARTS, MIX_W, P, {
        "rw1": twice(a["L1_ffn_router_w1"]), "ew1": twice(a["L1_ffn_expert_w1"].transpose(1, 0, 2).reshape(C, NE1 * C)),
        "ew2": diagonal(a["L1_ffn_expert_w2"]), "ew3": diagonal(a["L1_ffn_expert_w3"]),
        "eb1": by_pairs(a["L1_ffn_expert_b1"]), "eb2": by_pairs(a["L1_ffn_expert_b2"]),
        "rb1": col(a["L1_ffn_router_b1"]),
        "rw2": _np.concatenate([a["L1_ffn_router_w2"], a["L1_ffn_router_b2"][None]], axis=0)})

    arrays = {
        "x_row": a["x"].reshape(-1), "x_col": _np.ascontiguousarray(a["x"].T),
        "mask_col": _np.ascontiguousarray(a["mask_BS_i0_1"].T),
        "tokw": tokw, "attw": attw, "ffnw": ffnw, "w13": w13, "w2": w2, "mixw": mixw,
        "eb3": a["L1_ffn_expert_b3"].reshape(1, -1),
    }
    nc = _bacc.Bacc("TRN2", target_bir_lowering=False, num_devices=1)
    args = [nc.dram_tensor(n, v.shape, mybir.dt.from_np(v.dtype), kind="ExternalInput").ap() for n, v in arrays.items()]
    out = nc.dram_tensor("out", (NB, P, C), F32, kind="ExternalOutput").ap()
    tower_program(nc, *args, out)
    r = _run(nc, [arrays], core_ids=[0])
    return r.results[0]["out"]
```

```python
from collections import namedtuple
from contextlib import ExitStack

import numpy as np

import concourse.bass as bass
from concourse import mybir
from concourse.alu_op_type import AluOpType as ALU

ACT = mybir.ActivationFunctionType
AX = mybir.AxisListType
F32 = mybir.dt.float32
F32R = mybir.dt.float32r
BF16 = mybir.dt.bfloat16
I32 = mybir.dt.int32

P = 128
NB = 16
C = 64
GT = 4
NG = NB // GT
SKILLS = 75
LAND = 40
FEAT = 5
NH, NKV, HD = 4, 2, 16
NE0, HID = 8, 170
REM = HID - P
NCH = 11
NE1 = 6
EPS_LN, EPS_RMS = 1e-5, 1e-6
NEG = -3.0e38
MASKED = -1.0e30

CHUNKS = [("r", 0), ("f", 0), ("f", 1), ("f", 2), ("r", 1), ("f", 3), ("f", 4), ("f", 5), ("r", 2), ("f", 6), ("f", 7)]
PAIR_CHUNKS = [[0, 1, 2], [0, 3, 4, 5], [4, 6, 7], [8, 9, 10]]
PART_AFTER = [[(0, 0)], [(0, 1)], [(0, 2)], [(1, 0), (1, 3)], [(1, 4)], [(1, 5)], [(2, 4), (2, 6)], [(2, 7)], [(3, 8)], [(3, 9)],
              [(3, 10)]]
LAG0 = 2
LAST_PAIR = [n // 2 if kind == "f" else min(3 * n + 2, NE0 - 1) // 2 for kind, n in CHUNKS]
PIECE_AT = [0, 2, 8, 14, 21]
ROUTER_OPS = PIECE_AT[-1]
CONST_TOK, CONST_ALL = 11, 22


def layout_of(widths):
    at, out = 0, {}
    for name, width in widths:
        out[name] = (at, at + width)
        at += width
    return out, at


TOK_PARTS, TOK_W = layout_of([("p1", C), ("auga", P), ("augb", P)])
ATT_PARTS, ATT_W = layout_of([("wqT", C), ("wkT", C), ("wvT", C), ("woT", C), ("bq", 1), ("bk", 1), ("bv", 1),
                              ("l1wq", 2 * C), ("l1wk", C)])
FFN_PARTS, FFN_W = layout_of([("wqkv", 2 * C), ("wo", C), ("router", NE0), ("ln1", 1), ("ln2", 1),
                              ("cos", HD), ("sin", HD)])
MIX_PARTS, MIX_W = layout_of([("rw1", 32), ("ew1", NE1 * C), ("ew2", NE1 * C), ("ew3", NE1 * C), ("eb1", 3), ("eb2", 3),
                              ("rb1", 1), ("rw2", NE1)])


def bank_plan(order):
    uses = [("mct", 0, 1), ("qkv5", 1, 1), ("cnt", 3, 1), ("small", 2, 1),
            ("ut0", 4, 1), ("gram", 5, 1), ("gT", 7, 1), ("gsum", 0, 1), ("z", 1, 1), ("scT", 2, 1),
            ("posT", 3, 1), ("landq", 4, 1)]
    uses += [(("logit", k), [0, 5, 6, 7][k], 1) for k in range(4)]
    uses += [(("eqT", 0), 2, 1), (("eqT", 1), 3, 1), ("gb", 1, 1), ("a", 4, 1), ("ut1", 0, 1), (("h1", 0), 5, 1),
             (("h1", 1), 6, 1), ("l1a", 7, 1)]
    for step, g in order:
        if step == "F0e":
            uses.append((("xt", g), 0, 1))
        elif step == "F0d":
            uses.append((("qkv", g), 1, 2))
        elif step == "F1b":
            uses += [(("qT", g), 2, 1), (("kT", g), 3, 1)]
        elif step == "S":
            uses.append((("s",) + g, 4 + g[1] % 2, 1))
        elif step == "T":
            uses.append((("pT",) + g, 6, 1))
        elif step == "V" and g[1] == 0:
            uses.append((("y", g[0]), 7, 1))
        elif step == "F3b":
            uses.append((("proj", g), 3, 1))
        elif step == "F4e":
            uses.append((("xt2", g), 0, 1))
        elif step == "F4b":
            uses.append((("route", g), 1, 1))
        elif step == "M0":
            if g < NG * NCH:
                uses += [(("u1", g), 2 * (g % 2), 1), (("u3", g), 2 * (g % 2) + 1, 0)]
            uses += [(("pair", q, j), 4 + j % 2, 1) for q, j, n, first, last in parts_after(g - LAG0) if first]
        elif step == "A1c":
            uses.append((("x3T", g), 6, 1))
        elif step == "A1d":
            uses.append((("u", g), 7, 1))
        elif step == "A1e":
            uses.append((("sim", g), 6, 1))
        elif step == "A2b":
            uses.append((("p1T", g), 7, 1))
        elif step == "A2c":
            uses.append((("o1", g), 6, 1))
        elif step == "M1x":
            uses.append((("xt3", g), 7, 1))
        elif step == "M1d":
            uses.append((("rh", g), 6, 1))
        elif step == "M1e":
            uses.append((("route1", g), 7, 1))
        elif step == "L1":
            uses.append((("h1c",) + g, 2, 1))
        elif step == "L2":
            uses.append((("h2c",) + g, 3, 1))
        elif step == "L3":
            uses.append((("oc",) + g, (4, 1, 0, 5)[(3 * g[0] + g[1]) % 4], 1))
    bank, full, free, done = {}, {}, {}, {}
    written, read = [0] * 8, [0] * 8
    for key, b, readers in uses:
        assert key not in bank, key
        bank[key] = b
        free[key] = read[b]
        written[b] += 0 if key[0] == "y" else 1
        read[b] += readers
        full[key], done[key] = written[b], read[b]
    return bank, full, free, done


def parts_after(t):
    if not 0 <= t < NG * NCH:
        return []
    q, n = divmod(t, NCH)
    return [(q, j, c, c == PAIR_CHUNKS[j][0], c == PAIR_CHUNKS[j][-1]) for j, c in PART_AFTER[n]]


FIRST = {
    "F0a": -11.6, "F0b": -5.4,
    "F0c": 2.4, "F0e": 5.2, "F0d": 12.2,
    "F1a": 14.2, "F1b": 16.7,
    "S": 19.6, "N": 21.1, "T": 23.5, "V": 25.2,
    "F3a": 31.9, "F3b": 33,
    "F3c": 34.4, "F4a": 35.2, "F4e": 39.2, "R0": 47.1, "F4b": 45.8,
}
SECOND = {
    "A1a": 17.8, "A1b": 17.9, "A1c": 19.7, "A1d": 20.7, "A1e": 21.4,
    "A2a": 22, "A2b": 23.4, "A2c": 24.6,
    "M1a": 25.7, "M1b": 25.8, "M1c": 28.2, "M1x": 28.4, "M1d": 29.8, "M1e": 30.6, "R1": 32.8,
    "L1": 47, "L2": 50.7, "L3": 53.4, "W": 55.3, "Z": 64.4,
}


SPACING = {"first1": 8.5, "first2": 17, "first3": 25.5, "second1": 10.8, "second2": 21.6, "second3": 32.4,
           "third1": 6.9, "third2": 13.8, "third3": 20.3,
           "head": 2.2, "pair": 2.3, "chunk": 1, "piece": 0.9, "mix": 67.6}


def steps_in_order():
    steps = [(SPACING["mix"] + SPACING["chunk"] * t, "M0", t) for t in range(NG * NCH + LAG0 + 1)]
    for g in range(NG):
        first = SPACING[f"first{g}"] if g else 0
        second, third = (SPACING["mix"] + (SPACING[f"{kind}{g}"] if g else 0) for kind in ("second", "third"))
        for step, slot in FIRST.items():
            if step in "SNTV":
                steps += [(first + SPACING["head"] * h + slot, step, (g, h)) for h in range(NH)]
            elif step != "R0":
                steps.append((first + slot, step, g))
            elif g % 2:
                steps += [(first + SPACING["piece"] * k + slot, step, (g // 2, k)) for k in range(4)]
        for step, slot in SECOND.items():
            if step in ("L1", "L2", "L3", "W"):
                steps += [(third + SPACING["pair"] * c + slot, step, (g, c)) for c in range(3)]
            elif step == "Z":
                steps.append((third + slot, step, g))
            elif step != "R1":
                steps.append((second + slot, step, g))
            elif g % 2:
                steps += [(second + SPACING["piece"] * k + slot, step, (g // 2, k)) for k in range(4)]
    return [s[1:] for s in sorted(steps, key=lambda s: s[0])]


ORDER = steps_in_order()


def tower_program(nc, x_row, x_col, mask_col, tokw, attw, ffnw, w13, w2, mixw, eb3, out):
    bank, full, free, done = bank_plan(ORDER)
    ctx = ExitStack()
    with ctx:
        def sb(name, shape, dt=F32):
            return ctx.enter_context(nc.sbuf_tensor(name, shape, dt))

        xcol_i = sb("xcol_i", [P, NB], I32)
        mcol_i = sb("mcol_i", [P, NB], I32)
        tok_w = sb("tok_w", [C + 2, TOK_W])
        att_w = sb("att_w", [C, ATT_W])
        ffn_w = sb("ffn_w", [P, FFN_W])
        mix_w = sb("mix_w", [P, MIX_W])
        later = sb("later", [P, 7 * 512])
        w13_raw = later[:, 0:2 * NCH * P]
        w2_sb = sb("w2_sb", [P, 2 * 512])
        b3_raw = sb("b3_raw", [33, NE1 * C])

        arena = sb("arena", [P, 12 * 512])
        work = [arena[:, 512 * i:512 * i + 512] for i in range(12)]

        def early(lo, *shape):
            flat = arena[:, lo:lo + int(np.prod(shape))]
            if len(shape) == 2:
                return flat.rearrange("p (a b) -> p a b", a=shape[0])
            return flat

        ident = sb("ident", [P, P])
        ident_b = sb("ident_b", [P, P], BF16)
        ones = sb("ones", [P, P])
        causal_T = sb("causal_T", [P, P])
        neg_mask = sb("neg_mask", [P, GT, P], BF16)
        own_block = sb("own_block", [P, 8])
        own_quarter = sb("own_quarter", [P, GT])
        rank_iota = sb("rank_iota", [P, LAND])
        rev_iota = sb("rev_iota", [P, 8])
        half_neg = sb("half_neg", [P, NB])
        ones33 = sb("ones33", [33, P], F32R)

        p1c = sb("p1c", [C + 1, C])
        rowsum = sb("rowsum", [C + 1, 2])
        mct = sb("mct", [C, 4])
        qk5 = sb("qk5", [C, 2 * FEAT])
        k5_pad = sb("k5_pad", [C, GT, 32])
        v5_pad = sb("v5_pad", [C, 8, 16])
        k10 = sb("k10", [P, GT, 2 * FEAT])
        mct_pad = sb("mct_pad", [C, 8, 16])
        gram_blk = sb("gram_blk", [P, 8, 4])
        w16_blk = sb("w16_blk", [P, 8, C])
        l1a = sb("l1a", [P, C])
        qkv_s = sb("qkv_s", [P, 2 * C])
        qkv_h = sb("qkv_h", [P, 2 * C], F32R)
        qkv_l = sb("qkv_l", [P, 2 * C], F32R)
        rt_s = sb("rt_s", [P, NE0])
        rt_h = sb("rt_h", [P, NE0], F32R)
        rt_l = sb("rt_l", [P, NE0], F32R)
        w13_h = sb("w13_h", [P, 2 * NCH * P], F32R)
        w13_l = sb("w13_l", [P, 2 * NCH * P], F32R)
        ew_h = sb("ew_h", [P, 32 + NE1 * C], F32R)
        ew_l = sb("ew_l", [P, 32 + NE1 * C], F32R)
        b3_hl = sb("b3_hl", [33, NE1 * C], F32R)
        b3_h = sb("b3_h", [33, NE1 * C], F32R)

        h1 = sb("h1", [P, NB, C])
        h2 = sb("h2", [P, NB, C])
        h3 = sb("h3", [P, NB, C])
        xcol = sb("xcol", [P, NB])
        valid = sb("valid", [P, NB, 2])
        xrow_i = early(0, NB * P).bitcast(I32)
        same = early(2048, NB * P // 2).bitcast(BF16).rearrange("p (b t) -> p b t", b=NB)
        mcol = sb("mcol", [P, NB])
        mcol_rest = sb("mcol_rest", [P, 2, NB])
        one_r = sb("one_r", [P, NB, 4], BF16)
        cnt = sb("cnt", [P, NB, 2])
        mast = sb("mast", [P, NB, 2])
        feats = sb("feats", [P, NB, 16])
        feats_T = sb("feats_T", [P, 2, P])
        feats_T1 = sb("feats_T1", [P, 2, P])
        gram_f = sb("gram_f", [P, NB, 4])
        var0 = sb("var0", [P, NB])
        var0e = sb("var0e", [P, NB])
        inv0 = sb("inv0", [P, NB])
        g5 = h2[:, 0:8].rearrange("p a b -> p (a b)").rearrange("p (a b) -> p a b", b=32)
        g5_T = h2[:, 8:16].rearrange("p a b -> p (a b)").rearrange("p (a b) -> p a b", b=P)
        z = h3[:].rearrange("p a b -> p (a b)").rearrange("p (k a b) -> p k a b", k=2, b=32)
        zg = sb("zg", [P, NB, FEAT])
        score = sb("score", [P, NB])
        score_T = early(3584, 6, P)[0:NB]
        top8 = sb("top8", [NB, 5, 8])
        chosen = sb("chosen", [NB, P])
        ones16 = sb("ones16", [NB, P])
        count_T = sb("count_T", [NB, P])
        place_T = sb("place_T", [NB, P])
        pick = early(0, NB, LAND)
        lmax = sb("lmax", [P, GT, 8])
        lsub = early(2304, 32, LAND).rearrange("p (q r) l -> p q r l", q=NG)
        eq = early(5120, NB, 64)
        ek = early(640, NB, LAND)
        lsum = sb("lsum", [P, 2, NB])
        linv = sb("linv", [P, 2, NB])
        g5k = sb("g5k", [P, NB, FEAT])
        eq_T = early(1280, 8, P)
        gsum_l = sb("gsum_l", [P, 8, 2, FEAT])

        h12 = sb("h12", [P, NB, C])
        h4 = h12

        def per_group(name, shape, dt=F32):
            t = sb(name, [shape[0], NG] + shape[1:], dt)
            return [t[:, g] for g in range(NG)]

        nsum = [per_group(f"nsum{n}", [P, GT]) for n in range(4)]
        ncen = [per_group("ncen", [P, GT, C])] * 4
        nss = [per_group(f"nss{n}", [P, GT]) for n in range(4)]
        nve = [per_group(f"nve{n}", [P, 2, GT]) for n in range(4)]
        ninv = [per_group(f"ninv{n}", [P, 2, GT]) for n in range(4)]
        xhl = [per_group("xhl", [P, GT, 2, C], F32R)] * 3
        xT = [per_group(f"xT{n}", [P, GT, P], F32R) for n in range(2)]
        xT.append(xT[0])
        x2 = per_group("x2", [P, GT, C])
        shared = sb("shared", [P, 6 * 512])
        half = GT * 6 * HD
        rope1, rope2 = ([shared[:, half * (2 * (g % 2) + k):half * (2 * (g % 2) + k + 1)].rearrange("p (t h d) -> p t h d", t=GT, h=6)
                         for g in range(NG)] for k in range(2))
        y_blk = shared[:, 0:4 * GT * 2 * LAND].rearrange("p (q i l) -> p q i l", q=NG, i=GT)
        q_pad = [sb(f"q_pad{i}", [P, GT, NH, 32]) for i in range(2)]
        k_pad = [sb(f"k_pad{i}", [P, GT, NKV, 2, 32]) for i in range(2)]
        v_pad = per_group("v_pad", [P, GT, NKV, 32])
        qT = [sb(f"qT{i}", [P, GT, P]) for i in range(2)]
        kT_own = sb("kT_own", [P, 2 * 512])
        kT = [[later[:, 512 * h:512 * h + 512] for h in range(NH)],
              [kT_own[:, 0:512], kT_own[:, 512:1024], shared[:, 2048:2560], shared[:, 2560:3072]]]
        smax, smax_n, ssum, sinv = (per_group(n, [P, NH, GT]) for n in ("smax", "smax_n", "ssum", "sinv"))
        yT4 = [work[i].rearrange("p (t s) -> p t s", t=GT) for i in range(2)]
        expd = [work[4 + i].rearrange("p (t s) -> p t s", t=GT) for i in range(4)]
        probs_T = [work[8 + i].rearrange("p (t s) -> p t s", t=GT) for i in range(4)]
        ynorm = per_group("ynorm", [P, GT, C])
        yT = per_group("yT", [P, 2, P])
        nsq = [[v.rearrange("p a b -> p (a b)").rearrange("p (t c) -> p t c", t=GT) for v in yT]] * 4
        xs = [ynorm] * 3
        xres = ncen[0]

        route_cols = {n: sb(f"route_{n}", [P, NB]) for n in "lmax s inv best1 max2 best2 sum2 den deni".split()}
        route_rows = {n: sb(f"route_{n}", [P, NB, NE0])
                      for n in "logit lsub ex p eq1 key1 one1 rest eq2 key2 one2 both pw sub2 ex2 w".split()}

        RouterArrays = namedtuple("RouterArrays", [*route_cols, *route_rows])

        def router_set(e):
            return RouterArrays(*route_cols.values(), *(v[:, :, 0:e] for v in route_rows.values()))

        rs = [router_set(NE0), router_set(NE1)]

        gate = [later[:, 2048 + 512 * i:2560 + 512 * i] for i in range(3)]
        hid = work[0:NCH]
        weighted = [later[:, 512 * i:512 * i + 512].rearrange("p (t e c) -> p t e c", t=GT, e=2) for i in range(4)]
        acc = [shared[:, 512 * g:512 * g + 512].rearrange("p (t e c) -> p t e c", t=GT, e=2) for g in range(NG)]
        folded = [shared[:, 2048 + 256 * g:2304 + 256 * g].rearrange("p (t c) -> p t c", t=GT) for g in range(NG)]

        x3 = per_group("x3", [P, GT, C])
        x3T = [x2[g].rearrange("p t c -> p (t c)").rearrange("p (a b) -> p a b", a=2) for g in range(NG)]
        uT = yT
        m1, m1_n, e1_sum = (per_group(n, [P, GT]) for n in ("m1", "m1_n", "e1_sum"))
        e1 = [k_pad[i][:].rearrange("p t k r d -> p t (k r d)") for i in range(2)]
        p1T = qT
        o1inv = per_group("o1inv", [P, GT])
        o1 = ynorm
        rh = [sb(f"rh{i}", [33, 512])[:] for i in range(2)] * 2
        hid1 = work[6:8]
        hid2 = work[8:10]
        weighted1 = weighted
        acc1 = acc

        ps = [ctx.enter_context(nc.psum_tensor(f"bank{b}", [P, 512], F32)) for b in range(8)]

        def at(key):
            return ps[bank[key]]

        def sems(names):
            return namedtuple("Semaphores", names)(*(ctx.enter_context(nc.semaphore(n)) for n in names.split()))

        bank_full = [ctx.enter_context(nc.semaphore(f"bank_full{b}")) for b in range(8)]
        bank_free = [ctx.enter_context(nc.semaphore(f"bank_free{b}")) for b in range(8)]
        s = sems("tok_in tokw_in attw_in ffnw_in mixw_in w13_in w2_in b3_in stored "
                 "zeros shapes k_zero const p1c_ok k10_ok gram_ok gram_f_ok "
                 "folded_ok proj_hi proj_lo w13_scaled w13_hi w13_lo ew_hi ew_lo b3_hi "
                 "row_in0 row_in1 row_in2 row_in3 mask_in xc vld same_ok one_r_ok mst feats_ok var0_ok inv0_ok g5_ok "
                 "score_ok topk chosen_ok count_ok place_ok lmax_ok eexp lsum_ok linv_ok g5k_ok attended "
                 "nsum_ok ncen_ok nsq_ok nss_ok nve_ok ninv_ok xs_ok xhi_ok xlo_ok x2_ok "
                 "qkpad_ok smax_ok sinv_ok probs_ok pv_done "
                 "router0 router1 route_exp0 route_exp1 hid_ok acc0_ok acc1_ok h12_ok fold0_ok fold1_ok h2_ok "
                 "sim_half x3_ok m1_ok o1inv_ok h3_ok h4_ok")

        def wait_full(eng, key):
            eng.wait_ge(bank_full[bank[key]], full[key])

        def wait_free(eng, key):
            if free[key]:
                eng.wait_ge(bank_free[bank[key]], free[key])

        def wait_read(eng, key):
            eng.wait_ge(bank_free[bank[key]], done[key])

        def written(ins, key):
            ins.then_inc(bank_full[bank[key]], 1)

        def read(ins, key):
            ins.then_inc(bank_free[bank[key]], 1)

        def grp(t, g):
            return t[:, GT * g:GT * g + GT]

        def bc(ap, n):
            k = len(ap.shape)
            return ap.unsqueeze(k).to_broadcast(list(ap.shape) + [n])

        def bc_mid(ap, n):
            return ap.unsqueeze(1).to_broadcast([ap.shape[0], n] + list(ap.shape[1:]))

        def tokp(name, rows=C + 2):
            a, b = TOK_PARTS[name]
            return tok_w[0:rows, a:b]

        def attp(name):
            a, b = ATT_PARTS[name]
            return att_w[:, a:b]

        def ffnp(name):
            a, b = FFN_PARTS[name]
            return ffn_w[:, a:b]

        def mixp(name, rows=P):
            a, b = MIX_PARTS[name]
            return mix_w[0:rows, a:b]

        def turns(names):
            uses = [(names[step], g) for step, g in ORDER if step in names]
            return {k: n + 1 for n, k in enumerate(uses)}

        centre_turn = turns({"F0a": 0, "A1a": 2, "M1a": 3})
        square_turn = turns({"F0a": 0, "F3b": 1, "A1a": 2, "M1a": 3})
        norm_turn = turns({"F0b": 0, "F3c": 1, "A1b": 2, "M1b": 3})
        split_turn = turns({"F0c": 0, "F4a": 1, "M1c": 3})
        split_of = {0: 0, 1: 1, 3: 2}

        row_in = [s.row_in0, s.row_in1, s.row_in2, s.row_in3]

        block = ctx.enter_context(nc.Block())

        @block.sync
        def _(sp):
            sp.dma_start(xcol_i[:], x_col).then_inc(s.tok_in, 16)
            for q in range(NG):
                part = slice(GT * P * q, GT * P * (q + 1))
                sp.dma_start(xrow_i[:, part], x_row[part].partition_broadcast(P)).then_inc(row_in[q], 16)
            sp.dma_start(ffn_w[:], ffnw).then_inc(s.ffnw_in, 16)
            sp.dma_start(w13_raw, w13).then_inc(s.w13_in, 16)
            sp.dma_start(w2_sb[:], w2).then_inc(s.w2_in, 16)
            for step, g in ORDER:
                if step == "Z":
                    sp.wait_ge(s.h4_ok, g + 1)
                    sp.dma_start(out[GT * g:GT * g + GT].rearrange("b t c -> t b c"), grp(h4, g)).then_inc(s.stored, 16)
            sp.wait_ge(s.stored, 16 * NG)

        @block.gpsimd
        def _(pool):
            pool.dma_start(mcol_i[:], mask_col).then_inc(s.mask_in, 16)
            pool.memset(mct_pad[:], 0.0).then_inc(s.zeros, 1)
            pool.memset(ident[:], 0.0).then_inc(s.zeros, 1)
            pool.memset(ones[:], 1.0).then_inc(s.zeros, 1)
            pool.memset(neg_mask[:], 0.0).then_inc(s.zeros, 1)
            pool.memset(half_neg[:], -0.5).then_inc(s.zeros, 1)
            pool.wait_ge(s.zeros, 3)
            pool.affine_select(out=causal_T[:], in_=ones[:], compare_op=ALU.is_ge, fill=0.0, base=0,
                               pattern=[[1, P]], channel_multiplier=-1).then_inc(s.shapes, 1)
            pool.affine_select(out=ident[:], in_=ident[:], compare_op=ALU.not_equal, fill=1.0, base=0,
                               pattern=[[-1, P]], channel_multiplier=1).then_inc(s.shapes, 1)
            pool.affine_select(out=own_block[:], in_=ones[:, 0:8], compare_op=ALU.is_ge, fill=0.0, base=0,
                               pattern=[[-16, 8]], channel_multiplier=1).then_inc(s.shapes, 1)
            pool.affine_select(out=own_quarter[:], in_=ones[:, 0:GT], compare_op=ALU.is_ge, fill=0.0, base=0,
                               pattern=[[-32, GT]], channel_multiplier=1).then_inc(s.shapes, 1)
            pool.wait_ge(s.shapes, 4)
            pool.affine_select(out=own_block[:], in_=own_block[:], compare_op=ALU.is_ge, fill=0.0, base=15,
                               pattern=[[16, 8]], channel_multiplier=-1).then_inc(s.shapes, 1)
            pool.affine_select(out=own_quarter[:], in_=own_quarter[:], compare_op=ALU.is_ge, fill=0.0, base=31,
                               pattern=[[32, GT]], channel_multiplier=-1).then_inc(s.shapes, 1)
            pool.tensor_copy(ident_b[:], ident[:]).then_inc(s.const, 1)
            pool.wait_ge(s.zeros, 5)
            pool.affine_select(out=neg_mask[:], in_=neg_mask[:], compare_op=ALU.is_ge, fill=MASKED, base=0,
                               pattern=[[0, GT], [-1, P]], channel_multiplier=1).then_inc(s.const, 1)
            pool.iota(rank_iota[:], pattern=[[1, LAND]], base=1, channel_multiplier=0,
                      allow_small_or_imprecise_dtypes=True).then_inc(s.const, 1)
            pool.iota(rev_iota[:], pattern=[[-1, 8]], base=8, channel_multiplier=0,
                      allow_small_or_imprecise_dtypes=True).then_inc(s.const, 1)
            pool.tensor_copy(ones33[:], ones[0:33, :]).then_inc(s.const, 1)
            for t in (k5_pad[:], v5_pad[:], feats[:], g5, z, eq, gsum_l[:], q_pad[0][:], q_pad[1][:], k_pad[0][:], k_pad[1][:],
                      b3_raw[:], b3_hl[:].bitcast(F32)):
                pool.memset(t, 0.0).then_inc(s.const, 1)
            for g in range(NG):
                pool.memset(v_pad[g], 0.0).then_inc(s.const, 1)
            pool.wait_ge(s.const, CONST_ALL)
            for row in (0, 32):
                pool.dma_start(b3_raw[row:row + 1, :], eb3).then_inc(s.b3_in, 16)
            pool.wait_ge(s.var0_ok, 1)
            pool.tensor_tensor(inv0[:], var0e[:], half_neg[:], ALU.pow).then_inc(s.inv0_ok, 1)
            pool.memset(shared[:, 0:4 * GT * 2 * LAND], 0.0).then_inc(s.k_zero, 1)
            pool.memset(kT_own[:], 0.0).then_inc(s.k_zero, 1)
            pool.memset(shared[:, 2048:3072], 0.0).then_inc(s.k_zero, 1)

            def inverse_root(n, g):
                t = norm_turn[n, g]
                pool.wait_ge(s.nss_ok, t)
                eps = EPS_RMS if n == 1 else EPS_LN
                ins = pool.tensor_scalar(nve[n][g][:, 0], nss[n][g], 1.0 / C, eps, ALU.mult, ALU.add)
                if n == 0:
                    ins = pool.tensor_scalar(nve[n][g][:, 1], nss[n][g], (1.0 + EPS_RMS) / C, EPS_LN * EPS_RMS, ALU.mult,
                                             ALU.add)
                ins.then_inc(s.nve_ok, 1)
                pool.wait_ge(s.nve_ok, t)
                k = 2 if n == 0 else 1
                pool.tensor_tensor(ninv[n][g][:, 0:k].rearrange("p a b -> p (a b)"),
                                   nve[n][g][:, 0:k].rearrange("p a b -> p (a b)"),
                                   half_neg[:, 0:k * GT], ALU.pow).then_inc(s.ninv_ok, 1)

            pool.wait_ge(s.w13_lo, 2)
            pool.memset(later[:, 0:2048], 0.0).then_inc(s.k_zero, 1)
            for step, g in ORDER:
                if step == "F0b":
                    inverse_root(0, g)
                elif step == "F1a":
                    wait_read(pool, ("qkv", g))
                    if g >= 2:
                        wait_full(pool, ("qT", g - 2))
                        wait_full(pool, ("kT", g - 2))
                    pool.tensor_tensor(q_pad[g % 2][:, :, :, 0:HD], rope1[g][:, :, 0:NH], rope2[g][:, :, 0:NH], ALU.add)
                    for r in range(2):
                        ins = pool.tensor_tensor(k_pad[g % 2][:, :, :, r, 0:HD], rope1[g][:, :, NH:6], rope2[g][:, :, NH:6],
                                                 ALU.add)
                    ins.then_inc(s.qkpad_ok, 1)
                elif step == "F0c":
                    pool.wait_ge(s.ncen_ok, centre_turn[0, g])
                    pool.wait_ge(s.ninv_ok, norm_turn[0, g])
                    pool.tensor_tensor(x2[g], ncen[0][g], bc(ninv[0][g][:, 0], C), ALU.mult).then_inc(s.x2_ok, 1)
                elif step == "N":
                    g, h = g
                    t = NH * g + h
                    pool.wait_ge(s.sinv_ok, t + 1)
                    pool.tensor_tensor(expd[t % 4], expd[t % 4], bc(sinv[g][:, h], P), ALU.mult).then_inc(s.probs_ok, 1)
                elif step == "F3c":
                    inverse_root(1, g)
                    pool.tensor_tensor(grp(h12, g), grp(h1, g), xres[g], ALU.add).then_inc(s.h12_ok, 1)
                elif step == "M0":
                    for q, j, n, first, last in parts_after(g - LAG0 - 1):
                        if last and j:
                            wait_read(pool, ("pair", q, j))
                            if j > 1:
                                pool.wait_ge(s.acc0_ok, 3 * q + j - 1)
                            pool.tensor_tensor(acc[q], weighted[0] if j == 1 else acc[q], weighted[j],
                                               ALU.add).then_inc(s.acc0_ok, 1)
                elif step in ("A1b", "M1b"):
                    inverse_root(2 if step == "A1b" else 3, g)
                elif step == "A2c":
                    wait_read(pool, ("o1", g))
                    pool.tensor_tensor(grp(h3, g), grp(h2, g), o1[g], ALU.add).then_inc(s.h3_ok, 1)
                elif step == "W" and g[1]:
                    g, c = g
                    wait_read(pool, ("oc", g, c))
                    if c > 1:
                        pool.wait_ge(s.acc1_ok, 2 * g + c - 1)
                    pool.tensor_tensor(acc1[g], weighted1[0] if c == 1 else acc1[g], weighted1[c], ALU.add).then_inc(s.acc1_ok, 1)

        @block.scalar
        def _(act):
            act.dma_start(tok_w[:], tokw).then_inc(s.tokw_in, 16)
            act.dma_start(att_w[:], attw).then_inc(s.attw_in, 16)
            act.dma_start(mix_w[:], mixw).then_inc(s.mixw_in, 16)

            def copy(dst, src):
                return act.activation(dst, src, ACT.Copy)

            wait_full(act, "mct")
            copy(mct[:], at("mct")[0:C, 0:4])
            act.wait_ge(s.zeros, 1)
            read(copy(mct_pad[:, :, 0:4], bc_mid(at("mct")[0:C, 0:4], 8)), "mct")
            act.wait_ge(s.attw_in, 16)
            act.wait_ge(s.const, CONST_TOK)
            wait_full(act, "qkv5")
            q5, k5, v5 = (at("qkv5")[0:C, 8 * n:8 * n + 4] for n in range(3))
            copy(qk5[:, 0:4], q5)
            copy(qk5[:, 4:5], attp("bq"))
            copy(qk5[:, 5:9], k5)
            copy(qk5[:, 9:10], attp("bk"))
            copy(k5_pad[:, :, 0:4], bc_mid(k5, GT))
            copy(k5_pad[:, :, 4:5], bc_mid(attp("bk"), GT))
            copy(v5_pad[:, :, 12:13], bc_mid(attp("bv"), 8))
            read(copy(v5_pad[:, :, 8:12], bc_mid(v5, 8)), "qkv5")
            act.wait_ge(s.ffnw_in, 16)
            act.activation(qkv_s[:], ffnp("wqkv"), ACT.Copy, scale=ffnp("ln1"))
            act.activation(rt_s[:], ffnp("router"), ACT.Copy, scale=ffnp("ln2")).then_inc(s.folded_ok, 1)
            act.wait_ge(s.folded_ok, 1)
            copy(qkv_h[:], qkv_s[:])
            copy(rt_h[:], rt_s[:]).then_inc(s.proj_hi, 1)
            wait_full(act, "ut0")
            read(copy(feats_T[:].rearrange("p a b -> p (a b)"), at("ut0")[:, 0:2 * P]), "ut0")
            wait_full(act, "gT")
            read(copy(g5_T.rearrange("p a b -> p (a b)"), at("gT")[:]), "gT")
            act.wait_ge(s.w13_in, 16)
            for k in range(2):
                part = slice(k * NCH * P, (k + 1) * NCH * P)
                act.activation(w13_raw[:, part], w13_raw[:, part], ACT.Copy, scale=ffnp("ln2")).then_inc(s.w13_scaled, 1)
                act.wait_ge(s.w13_scaled, k + 1)
                copy(w13_h[:, part], w13_raw[:, part]).then_inc(s.w13_hi, 1)
            act.wait_ge(s.mixw_in, 16)
            copy(ew_h[:], mix_w[:, 0:32 + NE1 * C]).then_inc(s.ew_hi, 1)
            act.wait_ge(s.b3_in, 32)
            copy(b3_h[:], b3_raw[:]).then_inc(s.b3_hi, 1)
            wait_full(act, "landq")
            act.wait_ge(s.k_zero, 1)
            for i in range(GT):
                rows = slice(32 * i, 32 * i + 32)
                ins = copy(y_blk[rows, :, i], at("landq")[rows, 16:16 + GT * 2 * LAND].rearrange("p (q l) -> p q l", q=NG))
            read(ins, "landq")
            for q in range(NG):
                wait_read(act, ("logit", q))
                lv = lsub[:, q].rearrange("p (i two) l -> p i two l", two=2)
                act.activation(grp(ek, q), lv[:, :, 1], ACT.Exp, scale=0.125).then_inc(s.eexp, 1)
                act.activation(grp(eq, q)[:, :, 0:LAND], lv[:, :, 0], ACT.Exp, scale=0.125).then_inc(s.eexp, 1)
            for k in range(2):
                wait_full(act, ("eqT", k))
                read(copy(eq_T[:, 4 * k:4 * k + 4].rearrange("p a b -> p (a b)"), at(("eqT", k))[:]), ("eqT", k))
            wait_full(act, "ut1")
            read(copy(feats_T1[:].rearrange("p a b -> p (a b)"), at("ut1")[:, 0:2 * P]), "ut1")
            wait_full(act, ("h1", 1))
            read(copy(h1[:, 8:16].rearrange("p a b -> p (a b)"), at(("h1", 1))[:]), ("h1", 1))
            wait_full(act, "l1a")
            read(copy(l1a[:], at("l1a")[:, 0:C]), "l1a")

            def squares(n, g):
                if n == 1:
                    wait_read(act, ("proj", g))
                else:
                    act.wait_ge(s.ncen_ok, centre_turn[n, g])
                act.activation(nsq[n][g], xres[g] if n == 1 else ncen[n][g], ACT.Square).then_inc(s.nsq_ok, 1)

            def hi_part(n, g):
                k = split_of[n]
                act.wait_ge(s.xs_ok, split_turn[n, g])
                copy(xhl[k][g][:, :, 0], xs[k][g]).then_inc(s.xhi_ok, 1)

            def out_of(dst, key, cols=512):
                wait_full(act, key)
                read(copy(dst.rearrange("p a b -> p (a b)"), at(key)[:, 0:cols]), key)

            for step, g in ORDER:
                if step == "F0a":
                    squares(0, g)
                elif step == "F0c":
                    hi_part(0, g)
                elif step == "F0e":
                    out_of(xT[0][g], ("xt", g))
                elif step == "F0d":
                    wait_full(act, ("qkv", g))
                    if g == 0:
                        act.wait_ge(s.const, CONST_ALL)
                    vv = at(("qkv", g))[:].rearrange("p (t c) -> p t c", t=GT)[:, :, 96:128]
                    copy(v_pad[g][:, :, 0, 0:HD], vv[:, :, 0:HD])
                    read(copy(v_pad[g][:, :, 1, 0:HD], vv[:, :, HD:2 * HD]), ("qkv", g))
                elif step == "F1b":
                    wait_full(act, ("kT", g))
                    if g == 0:
                        act.wait_ge(s.k_zero, 4)
                    if g >= 2:
                        wait_full(act, ("s", g - 2, NH - 1))
                    for h in range(NH):
                        rows = slice(32 * h, 32 * h + 32)
                        ins = copy(kT[g % 2][h][rows, :], at(("kT", g))[rows, :])
                    read(ins, ("kT", g))
                elif step == "S":
                    g, h = g
                    t = NH * g + h
                    act.wait_ge(s.smax_ok, 2 * (t + 1))
                    if t >= 4:
                        wait_full(act, ("pT", g - 1, h))
                    for b in range(GT):
                        ins = act.activation(expd[t % 4][:, b], at(("s", g, h))[:, P * b:P * b + P], ACT.Exp, scale=HD ** -0.5,
                                             bias=smax_n[g][:, h, b:b + 1], accum_out=ssum[g][:, h, b:b + 1])
                    read(ins, ("s", g, h))
                elif step == "T":
                    t = NH * g[0] + g[1]
                    if t >= 4:
                        act.wait_ge(s.pv_done, t - 3)
                    out_of(probs_T[t % 4], ("pT",) + g)
                elif step == "F3a":
                    act.wait_ge(s.pv_done, NH * (g + 1))
                    if g >= 2:
                        wait_full(act, ("proj", g - 2))
                    read(copy(yT4[g % 2].rearrange("p a b -> p (a b)"), at(("y", g))[:]), ("y", g))
                elif step == "F3b":
                    squares(1, g)
                elif step == "F4a":
                    hi_part(1, g)
                elif step == "F4e":
                    out_of(xT[1][g], ("xt2", g))
                elif step == "R0" and g[1] == 0:
                    act.wait_ge(s.router0, ROUTER_OPS * g[0] + 2)
                    two = slice(2 * GT * g[0], 2 * GT * (g[0] + 1))
                    act.activation(rs[0].ex[:, two], rs[0].lsub[:, two], ACT.Exp).then_inc(s.route_exp0, 1)
                elif step == "M0":
                    if g < NG * NCH:
                        wait_full(act, ("u1", g))
                        if g >= 3:
                            act.wait_ge(s.hid_ok, g - 2)
                        read(act.activation(gate[g % 3], at(("u1", g))[:], ACT.Silu), ("u1", g))
                elif step == "A1a":
                    squares(2, g)
                elif step == "A1c":
                    out_of(x3T[g], ("x3T", g), 2 * P)
                elif step == "A1d":
                    out_of(uT[g], ("u", g), 2 * P)
                elif step == "A2a":
                    act.wait_ge(s.m1_ok, 2 * (g + 1))
                    if g >= 2:
                        wait_full(act, ("p1T", g - 2))
                    for i in range(GT):
                        ins = act.activation(e1[g % 2][:, i], at(("sim", g))[:, P * i:P * i + P], ACT.Exp, scale=0.125,
                                             bias=m1_n[g][:, i:i + 1], accum_out=e1_sum[g][:, i:i + 1])
                    read(ins, ("sim", g))
                elif step == "A2b":
                    if g >= 2:
                        wait_full(act, ("o1", g - 2))
                    out_of(p1T[g % 2][:], ("p1T", g))
                elif step == "M1a":
                    squares(3, g)
                elif step == "M1c":
                    hi_part(3, g)
                elif step == "M1x":
                    out_of(xT[2][g], ("xt3", g))
                elif step == "M1d":
                    wait_full(act, ("rh", g))
                    if g >= 2:
                        wait_full(act, ("route1", g - 2))
                    read(act.activation(rh[g][0:32, :], at(("rh", g))[0:32, :], ACT.Relu, bias=mixp("rb1", 32)), ("rh", g))
                elif step == "R1":
                    g, piece = g
                    two = slice(2 * GT * g, 2 * GT * (g + 1))
                    if piece == 0:
                        act.wait_ge(s.router1, ROUTER_OPS * g + 2)
                        act.activation(rs[1].ex[:, two], rs[1].lsub[:, two], ACT.Exp).then_inc(s.route_exp1, 1)
                    elif piece == 3:
                        act.wait_ge(s.router1, ROUTER_OPS * g + 16)
                        act.activation(rs[1].ex2[:, two], rs[1].sub2[:, two], ACT.Exp).then_inc(s.route_exp1, 1)
                elif step == "L1":
                    t = 3 * g[0] + g[1]
                    wait_full(act, ("h1c",) + g)
                    if t >= 2:
                        wait_full(act, ("h2c",) + divmod(t - 2, 3))
                    read(act.activation(hid1[t % 2], at(("h1c",) + g)[:], ACT.Relu, bias=mixp("eb1")[:, g[1]:g[1] + 1]),
                         ("h1c",) + g)

        @block.vector
        def _(dve):
            tt = dve.tensor_tensor
            for g in range(2):
                dve.memset(rh[g][32:33, :], 1.0)
            dve.wait_ge(s.tokw_in, 16)
            dve.tensor_reduce(rowsum[:, 0:1], tokp("p1", C + 1), AX.X, ALU.add).then_inc(s.p1c_ok, 1)
            dve.wait_ge(s.p1c_ok, 1)
            dve.tensor_scalar(rowsum[:, 1:2], rowsum[:, 0:1], -1.0 / C, None, ALU.mult).then_inc(s.p1c_ok, 1)
            dve.wait_ge(s.p1c_ok, 2)
            dve.tensor_scalar(p1c[:], tokp("p1", C + 1), rowsum[:, 1:2], None, ALU.add).then_inc(s.p1c_ok, 1)
            dve.wait_ge(s.mask_in, 16)
            dve.tensor_copy(mcol[:], mcol_i[:]).then_inc(s.one_r_ok, 1)
            dve.wait_ge(s.shapes, 6)
            dve.tensor_copy(one_r[:, :, 0], ones[:, 0:NB])
            rest = [mcol[:], mcol_rest[:, 0], mcol_rest[:, 1]]
            for k in range(3):
                dve.wait_ge(s.one_r_ok, 2 * k + 1)
                dve.tensor_copy(one_r[:, :, k + 1], rest[k]).then_inc(s.one_r_ok, 1)
                if k < 2:
                    dve.wait_ge(s.one_r_ok, 2 * k + 2)
                    tt(rest[k + 1], rest[k], one_r[:, :, k + 1], ALU.subtract).then_inc(s.one_r_ok, 1)
            dve.wait_ge(s.tok_in, 16)
            dve.tensor_copy(xcol[:], xcol_i[:]).then_inc(s.xc, 1)
            dve.wait_ge(s.xc, 1)
            for b in range(NB):
                if b % GT == 0:
                    dve.wait_ge(row_in[b // GT], 16)
                dve.scalar_tensor_tensor(out=same[:, b], in0=xrow_i[:, P * b:P * b + P], scalar=xcol[:, b:b + 1],
                                         in1=causal_T[:], op0=ALU.is_equal, op1=ALU.mult).then_inc(s.same_ok, 1)
            dve.tensor_scalar(valid[:, :, 0], xcol[:], 0.0, None, ALU.is_ge).then_inc(s.vld, 1)
            dve.wait_ge(s.vld, 1)
            dve.scalar_tensor_tensor(out=valid[:, :, 1], in0=xcol[:], scalar=float(SKILLS), in1=valid[:, :, 0],
                                     op0=ALU.is_lt, op1=ALU.mult).then_inc(s.vld, 1)
            dve.wait_ge(s.vld, 2)
            ok = valid[:, :, 1]
            dve.wait_ge(s.const, CONST_TOK)
            tt(feats[:, :, 0], xcol[:], ok, ALU.mult)
            dve.tensor_copy(feats[:, :, 3], ok)
            wait_full(dve, "cnt")
            cn = at("cnt")[:, 0:4 * NB].rearrange("p (b k) -> p b k", k=4)
            dve.tensor_copy(cnt[:, :, 0], cn[:, :, 0])
            read(dve.tensor_reduce(cnt[:, :, 1], cn[:, :, 1:4], AX.X, ALU.add), "cnt")
            wait_read(dve, "cnt")
            dve.tensor_scalar(mast[:, :, 0], cnt[:, :, 0], 1.0, None, ALU.max).then_inc(s.mst, 1)
            tt(feats[:, :, 1], cnt[:, :, 0], ok, ALU.mult)
            dve.wait_ge(s.mst, 1)
            dve.reciprocal(mast[:, :, 1], mast[:, :, 0]).then_inc(s.mst, 1)
            dve.wait_ge(s.mst, 2)
            tt(mast[:, :, 0], mast[:, :, 1], cnt[:, :, 1], ALU.mult).then_inc(s.mst, 1)
            dve.wait_ge(s.mst, 3)
            tt(feats[:, :, 2], mast[:, :, 0], ok, ALU.mult).then_inc(s.feats_ok, 1)
            wait_full(dve, "small")
            tt(k10[:], bc_mid(at("small")[:, 0:2 * FEAT], GT), bc(own_quarter[:], 2 * FEAT), ALU.mult).then_inc(s.k10_ok, 1)
            tt(gram_blk[:], bc_mid(at("small")[:, 16:20], 8), bc(own_block[:], 4), ALU.mult).then_inc(s.gram_ok, 1)
            wait_full(dve, "gram")
            read(tt(gram_f[:], at("gram")[:, 0:4 * NB].rearrange("p (b k) -> p b k", k=4), feats[:, :, 0:4], ALU.mult), "gram")
            wait_read(dve, "gram")
            dve.tensor_reduce(var0[:], gram_f[:], AX.X, ALU.add).then_inc(s.gram_f_ok, 1)
            dve.wait_ge(s.gram_f_ok, 1)
            dve.tensor_scalar(var0[:], var0[:], 0.0, 1.0 / C, ALU.max, ALU.mult).then_inc(s.gram_f_ok, 1)
            dve.wait_ge(s.gram_f_ok, 2)
            dve.tensor_scalar(var0e[:], var0[:], EPS_LN, None, ALU.add).then_inc(s.var0_ok, 1)
            read(tt(w16_blk[:], bc_mid(at("small")[:, 128:192], 8), bc(own_block[:], C), ALU.mult), "small")
            dve.wait_ge(s.proj_hi, 1)
            tt(qkv_l[:], qkv_s[:], qkv_h[:].bitcast(F32), ALU.subtract)
            tt(rt_l[:], rt_s[:], rt_h[:].bitcast(F32), ALU.subtract).then_inc(s.proj_lo, 1)
            dve.wait_ge(s.inv0_ok, 1)
            tt(g5[:, :, 0:4], feats[:, :, 0:4], bc(inv0[:], 4), ALU.mult)
            dve.memset(g5[:, :, 4:5], 1.0).then_inc(s.g5_ok, 1)
            dve.wait_ge(s.g5_ok, 1)
            dve.tensor_copy(feats[:, :, 4:8], g5[:, :, 0:4])
            wait_full(dve, "z")
            for k in range(2):
                ins = dve.tensor_copy(z[:, k, :, 0:FEAT],
                                      at("z")[:, 32:32 + 2 * FEAT * NB].rearrange("p (b c) -> p b c", b=NB)[:, :, FEAT * k:FEAT * k + FEAT])
            read(ins, "z")
            wait_read(dve, "z")
            wait_full(dve, "gsum")
            read(tt(zg[:], z[:, 0, :, 0:FEAT], at("gsum")[:, 0:FEAT * NB].rearrange("p (b c) -> p b c", b=NB), ALU.mult), "gsum")
            wait_read(dve, "gsum")
            dve.tensor_reduce(score[:], zg[:], AX.X, ALU.add).then_inc(s.score_ok, 1)
            wait_full(dve, "scT")
            read(dve.tensor_copy(score_T[:, 0], at("scT")[0:NB, 0:P]), "scT")
            wait_read(dve, "scT")
            for k in range(5):
                dve.max(top8[:, k], score_T[:, k]).then_inc(s.topk, 1)
                dve.wait_ge(s.topk, 2 * k + 1)
                dve.match_replace(score_T[:, k + 1], top8[:, k], score_T[:, k], NEG).then_inc(s.topk, 1)
                dve.wait_ge(s.topk, 2 * k + 2)
            dve.tensor_scalar(chosen[:], score_T[:, 5], NEG, None, ALU.is_equal).then_inc(s.chosen_ok, 1)
            dve.memset(ones16[:], 1.0).then_inc(s.chosen_ok, 1)
            dve.wait_ge(s.chosen_ok, 2)
            dve.tensor_tensor_scan(count_T[:], ones16[:], chosen[:], 0.0, ALU.mult, ALU.add).then_inc(s.count_ok, 1)
            dve.wait_ge(s.count_ok, 1)
            tt(place_T[:], count_T[:], chosen[:], ALU.mult).then_inc(s.place_ok, 1)
            wait_full(dve, "posT")
            read(tt(pick, bc_mid(rank_iota[:], NB), bc(at("posT")[:, 0:NB], LAND), ALU.is_equal), "posT")
            for k in range(2):
                part = slice(k * NCH * P, (k + 1) * NCH * P)
                dve.wait_ge(s.w13_hi, k + 1)
                tt(w13_l[:, part], w13_raw[:, part], w13_h[:, part].bitcast(F32), ALU.subtract).then_inc(s.w13_lo, 1)
            dve.wait_ge(s.ew_hi, 1)
            tt(ew_l[:], mix_w[:, 0:32 + NE1 * C], ew_h[:].bitcast(F32), ALU.subtract)
            dve.wait_ge(s.b3_hi, 1)
            dve.tensor_copy(b3_hl[0:1, :], b3_raw[0:1, :])
            tt(b3_hl[32:33, :], b3_raw[32:33, :], b3_h[32:33, :].bitcast(F32), ALU.subtract).then_inc(s.ew_lo, 1)
            for k in range(4):
                lg = at(("logit", k))[:, 0:GT * 2 * LAND].rearrange("p (r l) -> p r l", l=LAND)
                wait_full(dve, ("logit", k))
                dve.tensor_reduce(lmax[:, k], lg, AX.X, ALU.max).then_inc(s.lmax_ok, 1)
                dve.wait_ge(s.lmax_ok, k + 1)
                read(tt(lsub[:, k], lg, bc(lmax[:, k], LAND), ALU.subtract), ("logit", k))
            for k, e, exps in ((1, ek, 2 * NG - 1), (0, eq[:, :, 0:LAND], 2 * NG)):
                dve.wait_ge(s.eexp, exps)
                dve.tensor_reduce(lsum[:, k], e, AX.X, ALU.add).then_inc(s.lsum_ok, 1)
                dve.wait_ge(s.lsum_ok, 2 - k)
                dve.reciprocal(linv[:, k], lsum[:, k]).then_inc(s.linv_ok, 1)
                dve.wait_ge(s.linv_ok, 2 - k)
                if k:
                    tt(g5k[:], g5[:, :, 0:FEAT], bc(linv[:, 1], FEAT), ALU.mult).then_inc(s.g5k_ok, 1)
            wait_full(dve, "gb")
            for r in range(2):
                ins = dve.tensor_copy(gsum_l[64 * r:64 * r + LAND, :, r],
                                      at("gb")[64 * r:64 * r + LAND, 32:32 + 8 * FEAT].rearrange("p (a b) -> p a b", b=FEAT))
            read(ins, "gb")
            wait_full(dve, "a")
            read(tt(feats[:, :, 8:13], at("a")[:, 0:NB * FEAT].rearrange("p (b c) -> p b c", b=NB), bc(linv[:, 0], FEAT),
                    ALU.mult), "a")
            dve.memset(feats[:, :, 13:14], 1.0).then_inc(s.attended, 1)
            wait_full(dve, ("h1", 0))
            read(dve.tensor_copy(h1[:, 0:8].rearrange("p a b -> p (a b)"), at(("h1", 0))[:]), ("h1", 0))

            def centre(n, g, src):
                t = centre_turn[n, g]
                dve.tensor_reduce(nsum[n][g], src, AX.X, ALU.add).then_inc(s.nsum_ok, 1)
                dve.wait_ge(s.nsum_ok, t)
                dve.scalar_tensor_tensor(out=ncen[n][g], in0=bc(nsum[n][g], C), scalar=-1.0 / C, in1=src,
                                         op0=ALU.mult, op1=ALU.add).then_inc(s.ncen_ok, 1)

            def sum_squares(n, g):
                dve.wait_ge(s.nsq_ok, square_turn[n, g])
                dve.tensor_reduce(nss[n][g], nsq[n][g], AX.X, ALU.add).then_inc(s.nss_ok, 1)

            def scaled(n, g, src, row):
                dve.wait_ge(s.ninv_ok, norm_turn[n, g])
                tt(xs[split_of[n]][g], src, bc(ninv[n][g][:, row], C), ALU.mult).then_inc(s.xs_ok, 1)

            def lo_part(n, g):
                k = split_of[n]
                dve.wait_ge(s.xhi_ok, split_turn[n, g])
                tt(xhl[k][g][:, :, 1], xs[k][g], xhl[k][g][:, :, 0].bitcast(F32), ALU.subtract).then_inc(s.xlo_ok, 1)

            def logits_out(key, r, g, e, signal):
                wait_full(dve, key)
                signal(dve.tensor_copy(grp(r.logit, g), at(key)[:, 0:GT * e].rearrange("p (t e) -> p t e", e=e)), key)

            def route(lay, batch, piece, r, e):
                count = (s.router0, s.router1)[lay]
                place = [ROUTER_OPS * batch + PIECE_AT[piece]]
                lo, n = 2 * GT * batch, 2 * GT
                r = RouterArrays(*(v[:, lo:lo + n] for v in r))

                def link(ins):
                    place[0] += 1
                    ins.then_inc(count, 1)
                    dve.wait_ge(count, place[0])

                if piece == 0:
                    link(dve.tensor_reduce(r.lmax, r.logit, AX.X, ALU.max))
                    link(tt(r.lsub, r.logit, bc(r.lmax, e), ALU.subtract))
                elif piece == 1:
                    if lay:
                        dve.wait_ge(s.route_exp1, 2 * batch + 1)
                    else:
                        dve.wait_ge(s.route_exp0, batch + 1)
                    link(dve.tensor_reduce(r.s, r.ex, AX.X, ALU.add))
                    link(dve.reciprocal(r.inv, r.s))
                    link(tt(r.p, r.ex, bc(r.inv, e), ALU.mult))
                    link(tt(r.eq1, r.p, bc(r.inv, e), ALU.is_equal))
                    link(tt(r.key1, r.eq1, bc_mid(rev_iota[:, 0:e], n), ALU.mult))
                    link(dve.tensor_reduce(r.best1, r.key1, AX.X, ALU.max))
                elif piece == 2:
                    link(tt(r.one1, r.key1, bc(r.best1, e), ALU.is_equal))
                    link(dve.scalar_tensor_tensor(out=r.rest, in0=r.one1, scalar=-4.0, in1=r.p, op0=ALU.mult, op1=ALU.add))
                    link(dve.tensor_reduce(r.max2, r.rest, AX.X, ALU.max))
                    link(tt(r.eq2, r.rest, bc(r.max2, e), ALU.is_equal))
                    link(tt(r.key2, r.eq2, bc_mid(rev_iota[:, 0:e], n), ALU.mult))
                    link(dve.tensor_reduce(r.best2, r.key2, AX.X, ALU.max))
                else:
                    link(tt(r.one2, r.key2, bc(r.best2, e), ALU.is_equal))
                    if lay:
                        link(tt(r.sub2, r.p, bc(r.inv, e), ALU.subtract))
                        link(tt(r.both, r.one1, r.one2, ALU.add))
                        dve.wait_ge(s.route_exp1, 2 * batch + 2)
                        link(tt(r.pw, r.ex2, r.both, ALU.mult))
                        link(dve.tensor_reduce(r.den, r.pw, AX.X, ALU.add))
                    else:
                        link(tt(r.both, r.one1, r.one2, ALU.add))
                        link(tt(r.pw, r.p, r.both, ALU.mult))
                        link(dve.tensor_reduce(r.sum2, r.pw, AX.X, ALU.add))
                        link(dve.tensor_scalar(r.den, r.sum2, 1e-9, None, ALU.add))
                    link(dve.reciprocal(r.deni, r.den))
                    link(tt(r.w, r.pw, bc(r.deni, e), ALU.mult))
                assert place[0] == ROUTER_OPS * batch + PIECE_AT[piece + 1]

            def weigh(q, j):
                dve.wait_ge(s.router0, ROUTER_OPS * (q // 2 + 1))
                wait_full(dve, ("pair", q, j))
                if q >= 1:
                    dve.wait_ge(s.acc0_ok, 3 * (q - 1) + max(j, 1))
                read(tt(weighted[j], at(("pair", q, j))[:].rearrange("p (t e c) -> p t e c", t=GT, e=2),
                        bc(grp(rs[0].w, q)[:, :, 2 * j:2 * j + 2], C), ALU.mult), ("pair", q, j))

            def finish(q):
                dve.wait_ge(s.acc0_ok, 3 * (q + 1))
                tt(folded[q], acc[q][:, :, 0], acc[q][:, :, 1], ALU.add).then_inc(s.fold0_ok, 1)
                dve.wait_ge(s.fold0_ok, q + 1)
                dve.wait_ge(s.h12_ok, q + 1)
                tt(grp(h2, q), folded[q], grp(h12, q), ALU.add).then_inc(s.h2_ok, 1)

            def weigh1(g, c):
                dve.wait_ge(s.router1, ROUTER_OPS * (g // 2 + 1))
                wait_full(dve, ("oc", g, c))
                if g >= 1:
                    dve.wait_ge(s.acc1_ok, 2 * (g - 1) + max(c, 1))
                read(tt(weighted1[c], at(("oc", g, c))[:].rearrange("p (t e c) -> p t e c", t=GT, e=2),
                        bc(grp(rs[1].w, g)[:, :, 2 * c:2 * c + 2], C), ALU.mult), ("oc", g, c))

            for step, g in ORDER:
                if step == "F0a":
                    if g % 2 == 0:
                        wait_read(dve, ("h1", g // 2))
                    centre(0, g, grp(h1, g))
                elif step == "F0b":
                    sum_squares(0, g)
                elif step == "F0c":
                    scaled(0, g, ncen[0][g], 1)
                elif step == "F0e":
                    lo_part(0, g)
                elif step == "F1a":
                    dve.wait_ge(bank_free[bank["qkv", g]], done["qkv", g] - 1)
                    qk = at(("qkv", g))[:].rearrange("p (t h d) -> p t h d", t=GT, d=HD)[:, :, 0:6]
                    cos = bc_mid(bc_mid(ffnp("cos"), 6), GT)
                    sin = bc_mid(bc_mid(ffnp("sin"), 6), GT)
                    hh = HD // 2
                    if g >= 2:
                        dve.wait_ge(s.qkpad_ok, g - 1)
                    tt(rope1[g], qk, cos, ALU.mult)
                    tt(rope2[g][:, :, :, 0:hh], qk[:, :, :, hh:HD], sin[:, :, :, 0:hh], ALU.mult)
                    read(tt(rope2[g][:, :, :, hh:HD], qk[:, :, :, 0:hh], sin[:, :, :, hh:HD], ALU.mult), ("qkv", g))
                elif step == "F1b":
                    wait_full(dve, ("qT", g))
                    if g >= 2:
                        wait_full(dve, ("s", g - 2, NH - 1))
                    read(dve.tensor_copy(qT[g % 2][:].rearrange("p a b -> p (a b)"), at(("qT", g))[:]), ("qT", g))
                elif step == "S":
                    g, h = g
                    t = NH * g + h
                    wait_full(dve, ("s", g, h))
                    sc = at(("s", g, h))[:].rearrange("p (t s) -> p t s", t=GT)
                    dve.tensor_reduce(smax[g][:, h], sc, AX.X, ALU.max).then_inc(s.smax_ok, 1)
                    dve.wait_ge(s.smax_ok, 2 * t + 1)
                    dve.tensor_scalar(smax_n[g][:, h], smax[g][:, h], -HD ** -0.5, None, ALU.mult).then_inc(s.smax_ok, 1)
                elif step == "N":
                    g, h = g
                    wait_read(dve, ("s", g, h))
                    dve.reciprocal(sinv[g][:, h], ssum[g][:, h]).then_inc(s.sinv_ok, 1)
                elif step == "F3b":
                    wait_full(dve, ("proj", g))
                    dve.wait_ge(s.x2_ok, g + 1)
                    read(tt(xres[g], at(("proj", g))[:, 0:GT * C].rearrange("p (t c) -> p t c", t=GT), x2[g], ALU.add),
                         ("proj", g))
                elif step == "F3c":
                    sum_squares(1, g)
                elif step == "F4a":
                    scaled(1, g, xres[g], 0)
                elif step == "F4e":
                    lo_part(1, g)
                elif step == "F4b":
                    logits_out(("route", g), rs[0], g, NE0, read)
                elif step == "R0":
                    if g[1] == 0:
                        wait_read(dve, ("route", 2 * g[0] + 1))
                    route(0, *g, rs[0], NE0)
                elif step == "M0":
                    if g < NG * NCH:
                        q, n = divmod(g, NCH)
                        if q >= 1:
                            wait_full(dve, ("pair", q - 1, LAST_PAIR[n]))
                        wait_full(dve, ("u3", g))
                        wait_read(dve, ("u1", g))
                        tt(hid[n], at(("u3", g))[:], gate[g % 3], ALU.mult).then_inc(s.hid_ok, 1)
                    for q, j, n, first, last in parts_after(g - LAG0 - 1):
                        if last:
                            weigh(q, j)
                            if j == 0 and q:
                                finish(q - 1)
                    if g == NG * NCH + LAG0:
                        finish(NG - 1)
                elif step == "A1a":
                    dve.wait_ge(s.h2_ok, g + 1)
                    centre(2, g, grp(h2, g))
                elif step == "A1b":
                    sum_squares(2, g)
                elif step == "A1c":
                    dve.wait_ge(s.ninv_ok, norm_turn[2, g])
                    tt(x3[g], ncen[2][g], bc(ninv[2][g][:, 0], C), ALU.mult).then_inc(s.x3_ok, 1)
                elif step == "A2a":
                    wait_full(dve, ("sim", g))
                    sm = at(("sim", g))[:].rearrange("p (t s) -> p t s", t=GT)
                    dve.tensor_reduce(m1[g], sm, AX.X, ALU.max).then_inc(s.m1_ok, 1)
                    dve.wait_ge(s.m1_ok, 2 * g + 1)
                    dve.tensor_scalar(m1_n[g], m1[g], -0.125, None, ALU.mult).then_inc(s.m1_ok, 1)
                elif step == "A2c":
                    wait_read(dve, ("sim", g))
                    dve.reciprocal(o1inv[g], e1_sum[g]).then_inc(s.o1inv_ok, 1)
                    dve.wait_ge(s.o1inv_ok, g + 1)
                    wait_full(dve, ("o1", g))
                    oo = at(("o1", g))[:, 0:GT * C].rearrange("p (t c) -> p t c", t=GT)
                    read(tt(o1[g], oo, bc(o1inv[g], C), ALU.mult), ("o1", g))
                elif step == "M1a":
                    dve.wait_ge(s.h3_ok, g + 1)
                    centre(3, g, grp(h3, g))
                elif step == "M1b":
                    sum_squares(3, g)
                elif step == "M1c":
                    scaled(3, g, ncen[3][g], 0)
                elif step == "M1x":
                    lo_part(3, g)
                elif step == "M1e":
                    logits_out(("route1", g), rs[1], g, NE1, read)
                elif step == "R1":
                    if g[1] == 0:
                        wait_read(dve, ("route1", 2 * g[0] + 1))
                    route(1, *g, rs[1], NE1)
                elif step == "L2":
                    t = 3 * g[0] + g[1]
                    wait_full(dve, ("h2c",) + g)
                    if t >= 2:
                        wait_full(dve, ("oc",) + divmod(t - 2, 3))
                    read(dve.tensor_scalar(hid2[t % 2], at(("h2c",) + g)[:], mixp("eb2")[:, g[1]:g[1] + 1], 0.0, ALU.add,
                                           ALU.max), ("h2c",) + g)
                elif step == "W":
                    weigh1(*g)
                elif step == "Z":
                    dve.wait_ge(s.acc1_ok, 2 * (g + 1))
                    tt(folded[g], acc1[g][:, :, 0], acc1[g][:, :, 1], ALU.add).then_inc(s.fold1_ok, 1)
                    dve.wait_ge(s.fold1_ok, g + 1)
                    tt(grp(h4, g), folded[g], grp(h3, g), ALU.add).then_inc(s.h4_ok, 1)

        @block.tensor
        def _(pe):
            def mm(o, l, r, start=True):
                return pe.matmul(o, l, r, start=start, stop=True, skip_group_check=True)

            def rows_out(o, x, wh, wl, start=True):
                mm(o, x, wh, start=start)
                return mm(o, x, wl, start=False)

            def columns_out(o, wh, wl, x):
                mm(o, wh, x)
                return mm(o, wl, x, start=False)

            pe.wait_ge(s.p1c_ok, 3)
            a, _b = TOK_PARTS["augb"]
            written(mm(at("mct")[0:C, 0:4], p1c[:], tok_w[0:C + 1, a + 4:a + 8]), "mct")
            wait_read(pe, "mct")
            pe.wait_ge(s.attw_in, 16)
            for n, w in enumerate(("wqT", "wkT", "wvT")):
                ins = mm(at("qkv5")[0:C, 8 * n:8 * n + 4], attp(w), mct[:], start=(n == 0))
            written(ins, "qkv5")
            pe.wait_ge(s.one_r_ok, 6)
            for b in range(NB):
                pe.wait_ge(s.same_ok, b + 1)
                ins = mm(at("cnt")[:, 4 * b:4 * b + 4], same[:, b], one_r[:, b], start=(b == 0))
            written(ins, "cnt")
            wait_read(pe, "qkv5")
            sm = at("small")
            mm(sm[:, 16:20], mct_pad[:].rearrange("p a b -> p (a b)"), mct[:])
            mm(sm[:, 0:2 * FEAT], k5_pad[:].rearrange("p a b -> p (a b)"), qk5[:], start=False)
            mm(sm[:, 128:192], tokp("auga"), tokp("p1"), start=False)
            mm(sm[:, 128:192], tokp("augb", C + 1), p1c[:], start=False)
            written(mm(sm[:, 128:192], v5_pad[:].rearrange("p a b -> p (a b)"), attp("woT"), start=False), "small")
            pe.wait_ge(s.feats_ok, 1)
            for k in range(2):
                ins = pe.transpose(at("ut0")[:, P * k:P * k + P], feats[:, 8 * k:8 * k + 8].rearrange("p a b -> p (a b)"), ident[:])
            written(ins, "ut0")
            wait_read(pe, "ut0")
            pe.wait_ge(s.gram_ok, 1)
            for k in range(2):
                ins = mm(at("gram")[:, 32 * k:32 * k + 32], feats_T[:, k], gram_blk[:].rearrange("p a b -> p (a b)"), start=(k == 0))
            written(ins, "gram")
            pe.wait_ge(s.g5_ok, 1)
            for k in range(4):
                ins = pe.transpose(at("gT")[:, P * k:P * k + P], g5[:, GT * k:GT * k + GT].rearrange("p a b -> p (a b)"), ident[:])
            written(ins, "gT")
            wait_free(pe, "gsum")
            written(mm(at("gsum")[:, 0:FEAT * NB], ones[:], g5[:, :, 0:FEAT]), "gsum")
            wait_free(pe, "z")
            wait_read(pe, "gT")
            pe.wait_ge(s.k10_ok, 1)
            for q in range(NG):
                w = GT * 2 * FEAT
                ins = mm(at("z")[:, 32 + w * q:32 + w * (q + 1)], g5_T[:, q], k10[:].rearrange("p a b -> p (a b)"), start=(q == 0))
            written(ins, "z")
            pe.wait_ge(s.score_ok, 1)
            wait_free(pe, "scT")
            written(pe.transpose(at("scT")[0:NB, 0:P], score[:], ident[:]), "scT")
            pe.wait_ge(s.place_ok, 1)
            wait_free(pe, "posT")
            written(pe.transpose(at("posT")[:, 0:NB], place_T[:], ident[0:NB, 0:NB]), "posT")
            wait_free(pe, "landq")
            wait_read(pe, "posT")
            for b in range(NB):
                r = 32 * (b % GT)
                for k in range(2):
                    c0 = 16 + 2 * LAND * (b // GT) + LAND * k
                    ins = mm(at("landq")[r:r + 32, c0:c0 + LAND], z[:, k, b], pick[:, b])
            written(ins, "landq")
            wait_read(pe, "landq")
            for q in range(NG):
                wait_free(pe, ("logit", q))
                written(mm(at(("logit", q))[:, 0:GT * 2 * LAND], g5_T[:, q], y_blk[:, q].rearrange("p i l -> p (i l)")), ("logit", q))
            for k in range(2):
                pe.wait_ge(s.eexp, 4 * (k + 1))
                wait_free(pe, ("eqT", k))
                for j in range(4):
                    b = 8 * k + 2 * j
                    ins = pe.transpose(at(("eqT", k))[:, P * j:P * j + P], eq[:, b:b + 2].rearrange("p a b -> p (a b)"), ident[:])
                written(ins, ("eqT", k))
            pe.wait_ge(s.g5k_ok, 1)
            wait_free(pe, "gb")
            for b in range(NB):
                r = 64 * (b % 2)
                ins = mm(at("gb")[r:r + LAND, 32 + FEAT * (b // 2):32 + FEAT * (b // 2 + 1)], ek[:, b], g5k[:, b], start=(b < 2))
            written(ins, "gb")
            wait_read(pe, "gb")
            for k in range(2):
                wait_read(pe, ("eqT", k))
            wait_free(pe, "a")
            for b in range(0, NB, 2):
                ins = mm(at("a")[:, FEAT * b:FEAT * (b + 2)], eq_T[:, b // 2], gsum_l[:, b // 2].rearrange("p a b -> p (a b)"),
                         start=(b == 0))
            written(ins, "a")
            pe.wait_ge(s.attended, 1)
            wait_read(pe, "a")
            wait_free(pe, "ut1")
            for k in range(2):
                ins = pe.transpose(at("ut1")[:, P * k:P * k + P], feats[:, 8 * k:8 * k + 8].rearrange("p a b -> p (a b)"), ident[:])
            written(ins, "ut1")
            wait_read(pe, "ut1")
            for k in range(2):
                wait_free(pe, ("h1", k))
                written(mm(at(("h1", k))[:], feats_T1[:, k], w16_blk[:].rearrange("p a b -> p (a b)")), ("h1", k))
            wait_free(pe, "l1a")
            written(mm(at("l1a")[:, 0:C], attp("l1wq"), attp("l1wk")), "l1a")

            def stack_T(n, g, key):
                pe.wait_ge(s.xlo_ok, split_turn[n, g])
                wait_free(pe, key)
                for i in range(GT):
                    ins = pe.transpose(at(key)[:, P * i:P * i + P],
                                       xhl[split_of[n]][g][:, i].rearrange("p a b -> p (a b)").bitcast(F32), ident[:])
                written(ins, key)

            def part(q, j, n, first, last):
                key = ("pair", q, j)
                if first:
                    wait_free(pe, key)
                kind, m = CHUNKS[n]
                es = [m] if kind == "f" else [e for e in (2 * j, 2 * j + 1) if e // 3 == m]
                off = 0 if kind == "f" else 512
                for i in range(GT):
                    lo = 2 * C * i + C * (es[0] - 2 * j)
                    ins = mm(at(key)[:, lo:lo + C * len(es)], hid[n][:, P * i:P * i + P],
                             w2_sb[:, off + C * es[0]:off + C * (es[-1] + 1)], start=(first and i == 0))
                if last:
                    written(ins, key)

            def chunks_before(g):
                return sum(step == "M0" for step, _ in ORDER[:ORDER.index(("F4b", g))])

            for step, g in ORDER:
                if step == "F0e":
                    stack_T(0, g, ("xt", g))
                elif step == "F0d":
                    wait_read(pe, ("xt", g))
                    wait_free(pe, ("qkv", g))
                    if g == 0:
                        pe.wait_ge(s.proj_lo, 1)
                    for i in range(GT):
                        ins = rows_out(at(("qkv", g))[:, P * i:P * i + P], xT[0][g][:, i], qkv_h[:], qkv_l[:], start=(i == 0))
                    written(ins, ("qkv", g))
                elif step == "F1b":
                    pe.wait_ge(s.qkpad_ok, g + 1)
                    for key, src in ((("qT", g), q_pad[g % 2][:].rearrange("p t h d -> p t (h d)")),
                                     (("kT", g), k_pad[g % 2][:].rearrange("p t k r d -> p t (k r d)"))):
                        wait_free(pe, key)
                        for i in range(GT):
                            ins = pe.transpose(at(key)[:, P * i:P * i + P], src[:, i], ident[:])
                        written(ins, key)
                elif step == "S":
                    key, h = ("s",) + g, g[1]
                    g = g[0]
                    if h == 0:
                        wait_read(pe, ("qT", g))
                        wait_read(pe, ("kT", g))
                    if g == 0 and h == 0:
                        pe.wait_ge(s.const, CONST_ALL)
                    wait_free(pe, key)
                    mm(at(key)[:], ident_b[:], neg_mask[:].rearrange("p a b -> p (a b)"))
                    for b in range(GT):
                        ins = mm(at(key)[:, P * b:P * b + P], qT[g % 2][:, b], kT[g % 2][h][:, P * b:P * b + P], start=False)
                    written(ins, key)
                elif step == "T":
                    key, t = ("pT",) + g, NH * g[0] + g[1]
                    pe.wait_ge(s.probs_ok, t + 1)
                    wait_free(pe, key)
                    for b in range(GT):
                        ins = pe.transpose(at(key)[:, P * b:P * b + P], expd[t % 4][:, b], ident[:])
                    written(ins, key)
                elif step == "V":
                    wait_read(pe, ("pT",) + g)
                    g, h = g
                    if h == 0:
                        wait_free(pe, ("y", g))
                    for b in range(GT):
                        ins = mm(at(("y", g))[32 * h:32 * h + 32, P * b:P * b + P], v_pad[g][:, b, h // 2],
                                 probs_T[(NH * g + h) % 4][:, b], start=(b == 0))
                    ins.then_inc(s.pv_done, 1)
                elif step == "F3b":
                    wait_read(pe, ("y", g))
                    wait_free(pe, ("proj", g))
                    for i in range(GT):
                        ins = mm(at(("proj", g))[:, C * i:C * i + C], yT4[g % 2][:, i], ffnp("wo"), start=(i == 0))
                    written(ins, ("proj", g))
                elif step == "F4e":
                    stack_T(1, g, ("xt2", g))
                elif step == "F4b":
                    wait_read(pe, ("xt2", g))
                    wait_free(pe, ("route", g))
                    if chunks_before(g):
                        pe.wait_ge(s.hid_ok, (chunks_before(g) - 1) // 2 * 2 + 1)
                    for i in range(GT):
                        ins = rows_out(at(("route", g))[:, NE0 * i:NE0 * i + NE0], xT[1][g][:, i], rt_h[:], rt_l[:], start=(i == 0))
                    written(ins, ("route", g))
                elif step == "M0":
                    if g == 0:
                        pe.wait_ge(s.w13_lo, 2)
                        pe.wait_ge(s.w2_in, 16)
                    if g < NG * NCH:
                        q, n = divmod(g, NCH)
                        x = xT[1][q].rearrange("p a b -> p (a b)")
                        for u, off in (("u1", 0), ("u3", NCH * P)):
                            key = (u, g)
                            wait_free(pe, key)
                            if u == "u3" and g >= 2:
                                pe.wait_ge(s.hid_ok, g - 1)
                            cols = slice(off + P * n, off + P * n + P)
                            written(columns_out(at(key)[:], w13_h[:, cols], w13_l[:, cols], x), key)
                    todo = parts_after(g - LAG0)
                    if todo:
                        pe.wait_ge(s.hid_ok, g - LAG0 + 1)
                    for p in todo:
                        part(*p)
                elif step == "A1c":
                    key = ("x3T", g)
                    pe.wait_ge(s.x3_ok, g + 1)
                    wait_free(pe, key)
                    for i in range(2):
                        ins = pe.transpose(at(key)[:, P * i:P * i + P], x3[g][:, 2 * i:2 * i + 2].rearrange("p t c -> p (t c)"), ident[:])
                    written(ins, key)
                elif step == "A1d":
                    wait_read(pe, ("x3T", g))
                    if g == 0:
                        wait_read(pe, "l1a")
                    wait_free(pe, ("u", g))
                    for r in (0, C):
                        ins = mm(at(("u", g))[r:r + C, 0:2 * P], l1a[r:r + C, :], x3T[g][r:r + C].rearrange("p a b -> p (a b)"))
                    written(ins, ("u", g))
                elif step == "A1e":
                    wait_read(pe, ("u", g))
                    wait_free(pe, ("sim", g))
                    for i in (0, 2, 1, 3):
                        r = C * (i % 2)
                        if i == 1:
                            pe.wait_ge(s.sim_half, g + 1)
                        ins = mm(at(("sim", g))[:, P * i:P * i + P], uT[g][r:r + C, i // 2], x3T[g][r:r + C, i // 2], start=(i == 0))
                        if i == 2:
                            ins.then_inc(s.sim_half, 1)
                    written(ins, ("sim", g))
                elif step == "A2b":
                    key = ("p1T", g)
                    wait_read(pe, ("sim", g))
                    wait_free(pe, key)
                    for i in range(GT):
                        ins = pe.transpose(at(key)[:, P * i:P * i + P], e1[g % 2][:, i], ident[:])
                    written(ins, key)
                elif step == "A2c":
                    wait_read(pe, ("p1T", g))
                    wait_free(pe, ("o1", g))
                    for i in range(GT):
                        ins = mm(at(("o1", g))[:, C * i:C * i + C], p1T[g % 2][:, i], x3[g][:, i], start=(i == 0))
                    written(ins, ("o1", g))
                elif step == "M1x":
                    stack_T(3, g, ("xt3", g))
                elif step == "M1d":
                    wait_read(pe, ("xt3", g))
                    x = xT[2][g].rearrange("p a b -> p (a b)")
                    if g == 0:
                        pe.wait_ge(s.ew_lo, 1)
                    wait_free(pe, ("rh", g))
                    written(columns_out(at(("rh", g))[0:32, :], ew_h[:, 0:32], ew_l[:, 0:32], x), ("rh", g))
                elif step == "M1e":
                    wait_read(pe, ("rh", g))
                    wait_free(pe, ("route1", g))
                    for i in range(GT):
                        ins = mm(at(("route1", g))[:, NE1 * i:NE1 * i + NE1], rh[g][:, P * i:P * i + P], mixp("rw2", 33), start=(i == 0))
                    written(ins, ("route1", g))
                elif step == "L1":
                    key, c = ("h1c",) + g, g[1]
                    if c == 0:
                        wait_read(pe, ("xt3", g[0]))
                    wait_free(pe, key)
                    cols = slice(32 + P * c, 32 + P * c + P)
                    x = xT[2][g[0]].rearrange("p a b -> p (a b)")
                    written(columns_out(at(key)[:], ew_h[:, cols], ew_l[:, cols], x), key)
                elif step == "L2":
                    key, c = ("h2c",) + g, g[1]
                    wait_read(pe, ("h1c",) + g)
                    wait_free(pe, key)
                    written(mm(at(key)[:], mixp("ew2")[:, P * c:P * c + P], hid1[(3 * g[0] + c) % 2]), key)
                elif step == "L3":
                    key, c = ("oc",) + g, g[1]
                    wait_read(pe, ("h2c",) + g)
                    wait_free(pe, key)
                    mm(at(key)[:], ones33[:], bc_mid(b3_hl[:, P * c:P * c + P], GT))
                    for i in range(GT):
                        ins = mm(at(key)[:, P * i:P * i + P], hid2[(3 * g[0] + c) % 2][:, P * i:P * i + P],
                                 mixp("ew3")[:, P * c:P * c + P], start=False)
                    written(ins, key)



def kernel(**inputs):
    import numpy as _np
    import concourse.bacc as _bacc
    from concourse.bass_utils import run_bass_kernel_spmd as _run

    a = {k: _np.asarray(v) for k, v in inputs.items()}
    f32 = _np.float32

    def place(parts, width, rows, pieces):
        whole = _np.zeros((rows, width), f32)
        for name, piece in pieces.items():
            lo, hi = parts[name]
            whole[:piece.shape[0], lo:hi] = piece
        return whole

    def col(v):
        return v.reshape(-1, 1)

    def twice(m):
        return _np.concatenate([m, m], axis=0)

    d3 = a["L0_tok_skill_w"].shape[0]
    p1 = _np.concatenate([a["L0_tok_proj_w"].T, a["L0_tok_proj_b"][None], a["L0_attn_bo"][None]], axis=0)
    feat = _np.zeros((C + 2, 4), f32)
    feat[0:d3, 0] = a["L0_tok_skill_w"]
    feat[d3:2 * d3, 1] = a["L0_tok_att_w"]
    feat[2 * d3:C, 2] = a["L0_tok_mast_w"]
    feat[0:d3, 3] = a["L0_tok_skill_b"]
    feat[d3:2 * d3, 3] = a["L0_tok_att_b"]
    feat[2 * d3:C, 3] = a["L0_tok_mast_b"]
    feat[C, 3] = 1
    auga = _np.zeros((C + 2, 8, 16), f32)
    augb = _np.zeros((C + 2, 8, 16), f32)
    auga[:, :, 0:4] = feat[:, None, :]
    augb[:, :, 4:8] = feat[:, None, :]
    auga[C + 1, :, 13] = 1
    tokw = place(TOK_PARTS, TOK_W, C + 2, {"p1": p1, "auga": auga.reshape(C + 2, P), "augb": augb.reshape(C + 2, P)})

    attw = place(ATT_PARTS, ATT_W, C, {
        "wqT": a["L0_attn_Wq"].T, "wkT": a["L0_attn_Wk"].T, "wvT": a["L0_attn_Wv"].T, "woT": a["L0_attn_Wo"].T,
        "bq": col(a["L0_attn_bq"]), "bk": col(a["L0_attn_bk"]), "bv": col(a["L0_attn_bv"]),
        "l1wq": _np.concatenate([a["L1_attn_Wq"], a["L1_attn_Wq"]], axis=1), "l1wk": a["L1_attn_Wk"]})

    freq = 1.0 / 10000.0 ** (_np.arange(0, HD, 2, dtype=f32) / HD)
    angle = _np.outer(_np.arange(P, dtype=f32), freq)
    cos, sin = _np.cos(angle).astype(f32), _np.sin(angle).astype(f32)
    wo = _np.zeros((NH, 32, C), f32)
    wo[:, 0:HD] = a["L0_ffn_wo"].T.reshape(NH, HD, C)
    wo = wo.reshape(P, C)
    ffnw = place(FFN_PARTS, FFN_W, P, {
        "wqkv": twice(_np.concatenate([a["L0_ffn_wq"].T, a["L0_ffn_wk"].T, a["L0_ffn_wv"].T], axis=1)),
        "wo": wo, "router": twice(a["L0_ffn_router_w"].T),
        "ln1": twice(col(a["L0_ffn_ln1_w"])), "ln2": twice(col(a["L0_ffn_ln2_w"])),
        "cos": _np.concatenate([cos, cos], axis=1), "sin": _np.concatenate([-sin, sin], axis=1)})

    w13 = _np.zeros((C, 2, NCH, P), f32)
    for k, w in enumerate((a["L0_ffn_w1"], a["L0_ffn_w3"])):
        for n, (kind, m) in enumerate(CHUNKS):
            if kind == "f":
                w13[:, k, n] = w[m, 0:P].T
            else:
                for i, e in enumerate(range(3 * m, min(3 * m + 3, NE0))):
                    w13[:, k, n, REM * i:REM * i + REM] = w[e, P:HID].T
    w13 = twice(w13.reshape(C, 2 * NCH * P))
    w2 = _np.zeros((P, 2, NE0, C), f32)
    for e in range(NE0):
        w2[:, 0, e] = a["L0_ffn_w2"][e, :, 0:P].T
        w2[REM * (e % 3):REM * (e % 3) + REM, 1, e] = a["L0_ffn_w2"][e, :, P:HID].T
    w2 = w2.reshape(P, 2 * NE0 * C)

    def diagonal(w):
        blocks = _np.zeros((2, C, 3, 2, C), f32)
        for e in range(NE1):
            blocks[e % 2, :, e // 2, e % 2] = w[e]
        return blocks.reshape(P, NE1 * C)

    def by_pairs(b):
        return _np.ascontiguousarray(b.reshape(3, P).T)

    mixw = place(MIX_PARTS, MIX_W, P, {
        "rw1": twice(a["L1_ffn_router_w1"]), "ew1": twice(a["L1_ffn_expert_w1"].transpose(1, 0, 2).reshape(C, NE1 * C)),
        "ew2": diagonal(a["L1_ffn_expert_w2"]), "ew3": diagonal(a["L1_ffn_expert_w3"]),
        "eb1": by_pairs(a["L1_ffn_expert_b1"]), "eb2": by_pairs(a["L1_ffn_expert_b2"]),
        "rb1": col(a["L1_ffn_router_b1"]),
        "rw2": _np.concatenate([a["L1_ffn_router_w2"], a["L1_ffn_router_b2"][None]], axis=0)})

    arrays = {
        "x_row": a["x"].reshape(-1), "x_col": _np.ascontiguousarray(a["x"].T),
        "mask_col": _np.ascontiguousarray(a["mask_BS_i0_1"].T),
        "tokw": tokw, "attw": attw, "ffnw": ffnw, "w13": w13, "w2": w2, "mixw": mixw,
        "eb3": a["L1_ffn_expert_b3"].reshape(1, -1),
    }
    nc = _bacc.Bacc("TRN2", target_bir_lowering=False, num_devices=1)
    args = [nc.dram_tensor(n, v.shape, mybir.dt.from_np(v.dtype), kind="ExternalInput").ap() for n, v in arrays.items()]
    out = nc.dram_tensor("out", (NB, P, C), F32, kind="ExternalOutput").ap()
    tower_program(nc, *args, out)
    r = _run(nc, [arrays], core_ids=[0])
    return r.results[0]["out"]
```
